# Optimizing a Trainium2 kernel written in Bass

```python
import numpy as np
import jax
import jax.numpy as jnp

def _softmax(x, axis=-1):
    return jax.nn.softmax(x, axis=axis)

def _gelu(x):
    return jax.nn.gelu(x, approximate=True)

def _silu(x):
    return jax.nn.silu(x)

def _sigmoid(x):
    return jax.nn.sigmoid(x)

def _layernorm(x, axis=-1, eps=1e-05):
    m = jnp.mean(x, axis=axis, keepdims=True)
    v = jnp.var(x, axis=axis, keepdims=True)
    return (x - m) / jnp.sqrt(v + eps)

def _scatter_add(tgt, idx, src, axis=0):
    return tgt.at[idx].add(src)

def _segment_sum(src, seg, n):
    return jax.ops.segment_sum(src, seg, n)
kernel_name = 'mk_cond_seq_d2_seqx_r8_9f6b7b'

def setup_inputs(seed: int=0):
    np.random.seed(seed)
    _w = jnp.asarray

    def _rec_inputs():
        import jax
        import jax.numpy as jnp
        _rk = jax.random.key(seed)
        x = 7.22e-05 + 1 * jax.random.normal(jax.random.fold_in(_rk, 1), (128, 32, 128), jnp.float32)
        _lenS = 32 - jax.random.randint(jax.random.fold_in(_rk, 7), (128,), 0, max(1, 32 // 4) + 1, jnp.int32)
        _lenS2 = 32 - jax.random.randint(jax.random.fold_in(_rk, 8), (128,), 0, max(1, 32 // 4) + 1, jnp.int32)
        cond_1024 = 0.0061147 + 1.02565 * jax.random.normal(jax.random.fold_in(_rk, 11), (128, 128), jnp.float32)
        return (x, cond_1024)
    x, cond_1024 = _rec_inputs()

    def _L0_cond_setup():
        import jax, jax.numpy as jnp
        import numpy as np
        D = 128
        H = 16
        HD = D // H
        MLP = 4 * D

        def _lin(key, fin, fout):
            k1, k2 = jax.random.split(key)
            lim = 1.0 / np.sqrt(fin)
            W = jax.random.uniform(k1, (fin, fout), minval=-lim, maxval=lim, dtype=jnp.float32)
            b = jax.random.uniform(k2, (fout,), minval=-lim, maxval=lim, dtype=jnp.float32)
            return (W, b)

        def layernorm(x, g, b, eps=1e-05):
            mu = jnp.mean(x, axis=-1, keepdims=True)
            var = jnp.var(x, axis=-1, keepdims=True)
            return (x - mu) * jax.lax.rsqrt(var + eps) * g + b

        def attention(h, Wqkv, bqkv, Wproj, bproj):
            B, L, _ = h.shape
            qkv = (h @ Wqkv + bqkv).reshape(B, L, 3, H, HD)
            q, k, v = jnp.moveaxis(qkv, 2, 0)
            scale = HD ** (-0.5)
            attn = jnp.einsum('blhd,bmhd->bhlm', q, k) * scale
            attn = jax.nn.softmax(attn, axis=-1)
            out = jnp.einsum('bhlm,bmhd->blhd', attn, v).reshape(B, L, D)
            return out @ Wproj + bproj
        key = jax.random.key(seed)
        ks = jax.random.split(key, 10)
        x = jax.random.normal(ks[0], (4, 256, D), dtype=jnp.float32)
        time_emb = jax.random.normal(ks[1], (4, D), dtype=jnp.float32)
        Wqkv, bqkv = _lin(ks[2], D, 3 * D)
        Wproj, bproj = _lin(ks[3], D, D)
        W1, b1 = _lin(ks[4], D, MLP)
        W2, b2 = _lin(ks[5], MLP, D)
        Wt, bt = _lin(ks[6], D, 6 * D)
        g1 = jnp.ones((D,), jnp.float32)
        be1 = jnp.zeros((D,), jnp.float32)
        g2 = jnp.ones((D,), jnp.float32)
        be2 = jnp.zeros((D,), jnp.float32)
        return {'x': x, 'time_emb': time_emb, 'Wqkv': Wqkv, 'bqkv': bqkv, 'Wproj': Wproj, 'bproj': bproj, 'W1': W1, 'b1': b1, 'W2': W2, 'b2': b2, 'Wt': Wt, 'bt': bt, 'g1': g1, 'be1': be1, 'g2': g2, 'be2': be2}
    _L0_cond_all = _L0_cond_setup()
    _L0_cond_in = {k: v for k, v in _L0_cond_all.items() if k in ('Wqkv', 'bqkv', 'Wproj', 'bproj', 'W1', 'b1', 'W2', 'b2', 'Wt', 'bt', 'g1', 'be1', 'g2', 'be2')}
    del _L0_cond_all

    def _L1_cond_setup():
        import jax, jax.numpy as jnp
        import numpy as np
        DIM = 128
        MLP_RATIO = 4
        EPS = 1e-06

        def rmsnorm(x, w):
            return x * jax.lax.rsqrt(jnp.mean(x * x, axis=-1, keepdims=True) + EPS) * w

        def film(x, cond, w, b):
            ss = cond @ w + b
            scale, shift = jnp.split(ss, 2, axis=-1)
            return x * (1.0 + scale[:, None, :]) + shift[:, None, :]
        key = jax.random.key(seed)
        ks = jax.random.split(key, 16)
        B, N, D = (4, 256, DIM)
        H = D * MLP_RATIO
        s = lambda fan_in: 1.0 / np.sqrt(fan_in)
        return {'x': jax.random.normal(ks[0], (B, N, D), jnp.float32), 'cond': jax.random.normal(ks[1], (B, D), jnp.float32), 'norm1_w': jnp.ones((D,), jnp.float32), 'film1_w': jax.random.normal(ks[2], (D, 2 * D), jnp.float32) * s(D), 'film1_b': jnp.zeros((2 * D,), jnp.float32), 'q_w': jax.random.normal(ks[3], (D, D), jnp.float32) * s(D), 'q_b': jnp.zeros((D,), jnp.float32), 'k_w': jax.random.normal(ks[4], (D, D), jnp.float32) * s(D), 'k_b': jnp.zeros((D,), jnp.float32), 'v_w': jax.random.normal(ks[5], (D, D), jnp.float32) * s(D), 'v_b': jnp.zeros((D,), jnp.float32), 'proj_w': jax.random.normal(ks[6], (D, D), jnp.float32) * s(D), 'proj_b': jnp.zeros((D,), jnp.float32), 'norm2_w': jnp.ones((D,), jnp.float32), 'film2_w': jax.random.normal(ks[7], (D, 2 * D), jnp.float32) * s(D), 'film2_b': jnp.zeros((2 * D,), jnp.float32), 'mlp_w1': jax.random.normal(ks[8], (D, H), jnp.float32) * s(D), 'mlp_b1': jnp.zeros((H,), jnp.float32), 'mlp_w2': jax.random.normal(ks[9], (H, D), jnp.float32) * s(H), 'mlp_b2': jnp.zeros((D,), jnp.float32)}
    _L1_cond_all = _L1_cond_setup()
    _L1_cond_in = {k: v for k, v in _L1_cond_all.items() if k in ('norm1_w', 'film1_w', 'film1_b', 'q_w', 'q_b', 'k_w', 'k_b', 'v_w', 'v_b', 'proj_w', 'proj_b', 'norm2_w', 'film2_w', 'film2_b', 'mlp_w1', 'mlp_b1', 'mlp_w2', 'mlp_b2')}
    del _L1_cond_all
    return {'x': x, 'cond_1024': cond_1024, 'L0_cond_Wqkv': _L0_cond_in['Wqkv'], 'L0_cond_bqkv': _L0_cond_in['bqkv'], 'L0_cond_Wproj': _L0_cond_in['Wproj'], 'L0_cond_bproj': _L0_cond_in['bproj'], 'L0_cond_W1': _L0_cond_in['W1'], 'L0_cond_b1': _L0_cond_in['b1'], 'L0_cond_W2': _L0_cond_in['W2'], 'L0_cond_b2': _L0_cond_in['b2'], 'L0_cond_Wt': _L0_cond_in['Wt'], 'L0_cond_bt': _L0_cond_in['bt'], 'L0_cond_g1': _L0_cond_in['g1'], 'L0_cond_be1': _L0_cond_in['be1'], 'L0_cond_g2': _L0_cond_in['g2'], 'L0_cond_be2': _L0_cond_in['be2'], 'L1_cond_norm1_w': _L1_cond_in['norm1_w'], 'L1_cond_film1_w': _L1_cond_in['film1_w'], 'L1_cond_film1_b': _L1_cond_in['film1_b'], 'L1_cond_q_w': _L1_cond_in['q_w'], 'L1_cond_q_b': _L1_cond_in['q_b'], 'L1_cond_k_w': _L1_cond_in['k_w'], 'L1_cond_k_b': _L1_cond_in['k_b'], 'L1_cond_v_w': _L1_cond_in['v_w'], 'L1_cond_v_b': _L1_cond_in['v_b'], 'L1_cond_proj_w': _L1_cond_in['proj_w'], 'L1_cond_proj_b': _L1_cond_in['proj_b'], 'L1_cond_norm2_w': _L1_cond_in['norm2_w'], 'L1_cond_film2_w': _L1_cond_in['film2_w'], 'L1_cond_film2_b': _L1_cond_in['film2_b'], 'L1_cond_mlp_w1': _L1_cond_in['mlp_w1'], 'L1_cond_mlp_b1': _L1_cond_in['mlp_b1'], 'L1_cond_mlp_w2': _L1_cond_in['mlp_w2'], 'L1_cond_mlp_b2': _L1_cond_in['mlp_b2']}

def reference(x, cond_1024, L0_cond_Wqkv, L0_cond_bqkv, L0_cond_Wproj, L0_cond_bproj, L0_cond_W1, L0_cond_b1, L0_cond_W2, L0_cond_b2, L0_cond_Wt, L0_cond_bt, L0_cond_g1, L0_cond_be1, L0_cond_g2, L0_cond_be2, L1_cond_norm1_w, L1_cond_film1_w, L1_cond_film1_b, L1_cond_q_w, L1_cond_q_b, L1_cond_k_w, L1_cond_k_b, L1_cond_v_w, L1_cond_v_b, L1_cond_proj_w, L1_cond_proj_b, L1_cond_norm2_w, L1_cond_film2_w, L1_cond_film2_b, L1_cond_mlp_w1, L1_cond_mlp_b1, L1_cond_mlp_w2, L1_cond_mlp_b2):
    import jax
    import jax.numpy as jnp

    def _L0_cond_ref(x, time_emb, Wqkv, bqkv, Wproj, bproj, W1, b1, W2, b2, Wt, bt, g1, be1, g2, be2):
        import jax, jax.numpy as jnp
        import numpy as np
        D = 128
        H = 16
        HD = D // H
        MLP = 4 * D

        def _lin(key, fin, fout):
            k1, k2 = jax.random.split(key)
            lim = 1.0 / np.sqrt(fin)
            W = jax.random.uniform(k1, (fin, fout), minval=-lim, maxval=lim, dtype=jnp.float32)
            b = jax.random.uniform(k2, (fout,), minval=-lim, maxval=lim, dtype=jnp.float32)
            return (W, b)

        def layernorm(x, g, b, eps=1e-05):
            mu = jnp.mean(x, axis=-1, keepdims=True)
            var = jnp.var(x, axis=-1, keepdims=True)
            return (x - mu) * jax.lax.rsqrt(var + eps) * g + b

        def attention(h, Wqkv, bqkv, Wproj, bproj):
            B, L, _ = h.shape
            qkv = (h @ Wqkv + bqkv).reshape(B, L, 3, H, HD)
            q, k, v = jnp.moveaxis(qkv, 2, 0)
            scale = HD ** (-0.5)
            attn = jnp.einsum('blhd,bmhd->bhlm', q, k) * scale
            attn = jax.nn.softmax(attn, axis=-1)
            out = jnp.einsum('bhlm,bmhd->blhd', attn, v).reshape(B, L, D)
            return out @ Wproj + bproj
        tp = (jax.nn.silu(time_emb) @ Wt + bt)[:, None, :]
        shift_msa, scale_msa, gate_msa, shift_mlp, scale_mlp, gate_mlp = jnp.split(tp, 6, axis=-1)
        h = layernorm(x, g1, be1)
        h = h * (1.0 + scale_msa) + shift_msa
        h = attention(h, Wqkv, bqkv, Wproj, bproj)
        x = x + gate_msa * h
        h = layernorm(x, g2, be2)
        h = h * (1.0 + scale_mlp) + shift_mlp
        h = jax.nn.gelu(h @ W1 + b1, approximate=False) @ W2 + b2
        x = x + gate_mlp * h
        return x

    def _L1_cond_ref(x, cond, norm1_w, film1_w, film1_b, q_w, q_b, k_w, k_b, v_w, v_b, proj_w, proj_b, norm2_w, film2_w, film2_b, mlp_w1, mlp_b1, mlp_w2, mlp_b2):
        import jax, jax.numpy as jnp
        import numpy as np
        DIM = 128
        MLP_RATIO = 4
        EPS = 1e-06

        def rmsnorm(x, w):
            return x * jax.lax.rsqrt(jnp.mean(x * x, axis=-1, keepdims=True) + EPS) * w

        def film(x, cond, w, b):
            ss = cond @ w + b
            scale, shift = jnp.split(ss, 2, axis=-1)
            return x * (1.0 + scale[:, None, :]) + shift[:, None, :]
        B, N, D = x.shape
        x_in = x
        h = film(rmsnorm(x, norm1_w), cond, film1_w, film1_b)
        Q = h @ q_w + q_b
        K = h @ k_w + k_b
        V = h @ v_w + v_b
        scores = jnp.einsum('bnd,bmd->bnm', Q, K) * D ** (-0.5)
        attn = jax.nn.softmax(scores, axis=-1)
        out = jnp.einsum('bnm,bmd->bnd', attn, V)
        x = x_in + (out @ proj_w + proj_b)
        x_in = x
        h = film(rmsnorm(x, norm2_w), cond, film2_w, film2_b)
        h = jax.nn.gelu(h @ mlp_w1 + mlp_b1, approximate=False) @ mlp_w2 + mlp_b2
        return x_in + h
    x = _L0_cond_ref(x, cond_1024, L0_cond_Wqkv, L0_cond_bqkv, L0_cond_Wproj, L0_cond_bproj, L0_cond_W1, L0_cond_b1, L0_cond_W2, L0_cond_b2, L0_cond_Wt, L0_cond_bt, L0_cond_g1, L0_cond_be1, L0_cond_g2, L0_cond_be2)
    x = _L1_cond_ref(x, cond_1024, L1_cond_norm1_w, L1_cond_film1_w, L1_cond_film1_b, L1_cond_q_w, L1_cond_q_b, L1_cond_k_w, L1_cond_k_b, L1_cond_v_w, L1_cond_v_b, L1_cond_proj_w, L1_cond_proj_b, L1_cond_norm2_w, L1_cond_film2_w, L1_cond_film2_b, L1_cond_mlp_w1, L1_cond_mlp_b1, L1_cond_mlp_w2, L1_cond_mlp_b2)
    return x

_drawn_inputs = setup_inputs


def setup_inputs(seed=0):
    import zlib

    import numpy as np

    out = dict(_drawn_inputs(seed))
    spreads = {'L0_cond_g1': (1.0, 0.6),
     'L0_cond_be1': (0.0, 0.592),
     'L0_cond_g2': (1.0, 0.6),
     'L0_cond_be2': (0.0, 0.8),
     'L1_cond_norm1_w': (1.0, 0.2),
     'L1_cond_film1_b': (0.0, 0.1),
     'L1_cond_q_b': (0.0, 0.1),
     'L1_cond_k_b': (0.0, 0.8),
     'L1_cond_v_b': (0.0, 0.1),
     'L1_cond_proj_b': (0.0, 0.1),
     'L1_cond_norm2_w': (1.0, 0.2),
     'L1_cond_film2_b': (0.0, 0.1),
     'L1_cond_mlp_b1': (0.0, 0.1),
     'L1_cond_mlp_b2': (0.0, 0.1)}
    factors = {'L0_cond_bqkv': 4.129, 'L0_cond_b1': 7.006, 'L0_cond_b2': 5.192, 'L0_cond_bt': 2.788}
    for name, (base, spread) in spreads.items():
        noise = np.random.default_rng([zlib.crc32(name.encode()), seed]).standard_normal(out[name].shape)
        drawn = base * np.exp(spread * noise) if base else spread * noise
        out[name] = jnp.asarray(drawn.astype(out[name].dtype))
    for name, factor in factors.items():
        out[name] = (out[name] * factor).astype(out[name].dtype)
    return out
```

```python
from contextlib import ExitStack

import concourse.bass as bass
from concourse import mybir

F32 = mybir.dt.float32
ALU = mybir.AluOpType
ACT = mybir.ActivationFunctionType
AX_X = mybir.AxisListType.X

P = 128
D = 128
NB = 128
L = 32
H, HD = 16, 8
FF = 512
NC = FF // P
TB = P // L
NT = NB * L // P
TG = 4
NG = NT // TG
GB = TG * TB
GN = TG * P
HQ = 4
VW = HD + 1
OW = H * VW
SCALE0 = HD ** -0.5
SCALE1 = D ** -0.5
OFF_BLOCK = -1.0e30

W_NAMES = [("Wt", 6 * D), ("film1", 2 * D), ("film2", 2 * D), ("Wproj", D), ("v1", D), ("proj1", D),
           ("Wqkv", 3 * D), ("W1_0", FF), ("W2_0", FF), ("q1", D), ("k1", D), ("W1_1", FF), ("W2_1", FF)]
W_AT, W_ALL = {}, 0
for _name, _n in W_NAMES:
    W_AT[_name] = (W_ALL, _n)
    W_ALL += _n
C_NAMES = [("bt", 6), ("g1", 1), ("be1", 1), ("g2", 1), ("be2", 1), ("bq", 1), ("bk", 1), ("bv", 1), ("b1_0", NC),
           ("n1", 1), ("n2", 1), ("f1b", 2), ("f2b", 2), ("q1b", 1), ("k1b", 1), ("v1b", 1), ("b1_1", NC)]
C_AT, C_ALL = {}, 0
for _name, _n in C_NAMES:
    C_AT[_name] = (C_ALL, _n)
    C_ALL += _n
R_NAMES = ["gate0", "gate1", "bproj0", "b2_0", "bproj1", "b2_1"]


def build(nc, x, cond, weights, columns, rows, out):
    with ExitStack() as ctx:
        def sb(name, shape):
            return ctx.enter_context(nc.sbuf_tensor(name, shape, F32))

        def sem(name):
            return ctx.enter_context(nc.semaphore(name))

        gates_d = nc.dram_tensor("gates_scratch", [NB, 2 * D], F32, kind="Internal").ap()

        X = sb("X", [P, NT, D])
        gate = sb("gate", [P, NT, 2 * D])
        W = sb("W", [P, W_ALL])
        col = sb("col", [P, C_ALL])
        row = sb("row", [P, len(R_NAMES), D])
        c_tok, e_tok, s_tok = sb("c_tok", [NB, D]), sb("e_tok", [NB, D]), sb("s_tok", [NB, D])
        cT, sT = sb("cT", [D, NB]), sb("sT", [D, NB])
        A, B = sb("A", [D, 4 * NB]), sb("B", [D, 4 * NB])
        t_mul, one_plus = sb("t_mul", [D, NB]), sb("one_plus", [D, 8])
        gate_b = sb("gate_b", [NB, 2 * D])
        vT, wvp, bcol = sb("vT", [D, D]), sb("wvp", [D, D]), sb("bcol", [D, 2, D])
        q_bias = sb("q_bias", [D, 1])
        ident, mask, minus_half = (
            sb("ident", [P, P]), sb("mask", [P, P]), sb("minus_half", [P, TG]))
        kind = sb("kind", [P, 3, 4 * NG])
        stats, mv = sb("stats", [P, TG, 6]), sb("mv", [P, TG, 2])
        v_sb, mk, rstd, shift = (sb(n, [P, 2, TG]) for n in ("v_sb", "mk", "rstd", "shift"))
        sqm = sb("sqm", [P, TG])
        xhat = sb("xhat", [P, 2, GN])
        hA, h = sb("hA", [P, 2, GN]), sb("h", [P, 2, GN])
        Qs, Ks = sb("Qs", [P, 2, GN]), sb("Ks", [P, 2, GN])
        Vs = sb("Vs", [P, 2, TG * OW])
        Qx = sb("Qx", [P, 2, GB, HQ, L])
        Kx = sb("Kx", [P, 2, HQ, GN])
        Vx = sb("Vx", [P, 2, GB, HQ, HQ * VW])
        smax = sb("smax", [P, 2, TB * HQ])
        Ss, St = sb("Ss", [P, 2, GN]), sb("St", [P, 2, GN])
        PT = sb("PT", [P, TG, GN])
        rden, On, OTs = sb("rden", [P, 2 * H]), sb("On", [P, 2, GN]), sb("OTs", [P, 2, GN])
        xg, yG, gb = sb("xg", [P, 2, GN]), sb("yG", [P, GN]), sb("gb", [P, GN])
        max1, nmax1 = sb("max1", [P, TG]), sb("nmax1", [P, 2, TG])
        den1, rden1 = sb("den1", [P, 2, TG]), sb("rden1", [P, TG])
        gT = Qx[:, :, :, :, :].rearrange("p v (n b) a t -> p v n (b a t)", n=NC)

        bank = [ctx.enter_context(nc.psum_tensor(f"bank{i}", [P, 512], F32)) for i in range(8)]
        hT_ps, y_ps = bank[0], bank[1]

        x_in = [sem(f"x_in{i}") for i in range(5)]
        cond_in, col_in, wt_in, wrest_in, wmlp_in = (sem(n) for n in ("cond_in", "col_in", "wt_in", "wrest_in", "wmlp_in"))
        consts_ready, zeros_ready = sem("consts_ready"), sem("zeros_ready")
        exp_c, silu_ready, dve_pre = sem("exp_c"), sem("silu_ready"), sem("dve_pre")
        condT_ready, condT_copied = sem("condT_ready"), sem("condT_copied")
        film_ready, gate_ready, ab_ready = sem("film_ready"), sem("gate_ready"), sem("ab_ready")
        gates_stored, gates_in = sem("gates_stored"), sem("gates_in")
        fold_ready, fold_copied, rows_ready = sem("fold_ready"), sem("fold_copied"), sem("rows_ready")
        stats_done, mv_done, v_ready, rstd_ready = sem("stats_done"), sem("mv_done"), sem("v_ready"), sem("rstd_ready")
        pool_chain, dve_chain = sem("pool_chain"), sem("dve_chain")
        xhat_ready, hT_ready, hA_ready, h_ready = (
            sem(n) for n in ("xhat_ready", "hT_ready", "hA_ready", "h_ready"))
        gb_ready, xg_ready, y_ready, y_used, x_updated = (
            sem(n) for n in ("gb_ready", "xg_ready", "y_ready", "y_used", "x_updated"))
        qkv_ready, qkv_moved = sem("qkv_ready"), sem("qkv_moved")
        qk_spread = [sem(f"qk_spread{i}") for i in range(2)]
        v_spread = [sem(f"v_spread{i}") for i in range(2)]
        s_ready, smax_ready, s_used, st_ready, pt_ready, pv_done = (
            sem(n) for n in ("s_ready", "smax_ready", "s_used", "st_ready", "pt_ready", "pv_done"))
        rden_ready, o_used, ot_ready, ot_moved = (sem(n) for n in ("rden_ready", "o_used", "ot_ready", "ot_moved"))
        qkv1_ready, qkv1_moved, s1_ready, s1_masked, max1_ready, sm1_ready, p1_ready, p1T_ready, p1T_moved, rden1_ready = (
            sem(n) for n in ("qkv1_ready", "qkv1_moved", "s1_ready", "s1_masked", "max1_ready", "sm1_ready", "p1_ready", "p1T_ready",
                             "p1T_moved", "rden1_ready"))
        u_ready, g_ready = sem("u_ready"), sem("g_ready")
        out_done = sem("out_done")

        QK_DMAS, V_DMAS = HQ + H, TB * HQ
        UNTIL7 = NG - 1

        def w(name, i=0, n=D):
            at = W_AT[name][0] + i * n
            return W[:, at:at + n]

        def c(name, i=0):
            at = C_AT[name][0] + i
            return col[:, at:at + 1]

        def r(name):
            return row[:, R_NAMES.index(name), :]

        def by_tile(ap):
            return ap.rearrange("p (t d) -> p t d", t=TG)

        def by_seq(ap):
            return ap.rearrange("p (b t) -> p b t", t=L)

        def wait(eng, s, n):
            if not isinstance(n, int) or n > 0:
                eng.wait_ge(s, n)

        def group_steps(eng, step, last_loop=6):
            step(0, 0)
            with eng.Fori(0, last_loop // 2) as i:
                step(i * 2 + 1, 1)
                step(i * 2 + 2, 0)
            for g in range(last_loop + 1, NG):
                step(g, g % 2)

        def x_group(gg):
            if isinstance(gg, int):
                g = gg % NG
                return slice(g * TG, (g + 1) * TG)
            return bass.ds(((gg) % NG) * TG, TG)

        def x_tile(gg, t):
            if isinstance(gg, int):
                return slice((gg % NG) * TG + t, (gg % NG) * TG + t + 1)
            return bass.ds((gg % NG) * TG + t, 1)

        def seqs(gg):
            if isinstance(gg, int):
                return slice(gg * GB, (gg + 1) * GB)
            return bass.ds(gg * GB, GB)

        def one(gg):
            return slice(gg, gg + 1) if isinstance(gg, int) else bass.ds(gg, 1)

        block = ctx.enter_context(nc.Block())

        @block.sync
        def _(sp):
            xv = x.rearrange("(i p) d -> p i d", p=P)
            ov = out.rearrange("(i p) d -> p i d", p=P)
            sp.dma_start(c_tok[:, :], cond).then_inc(cond_in, 16)
            for g in range(4):
                sp.dma_start(X[:, TG * g:TG * (g + 1), :], xv[:, TG * g:TG * (g + 1), :]).then_inc(x_in[g], 16)
            sp.dma_start(X[:, 4 * TG:, :], xv[:, 4 * TG:, :]).then_inc(x_in[4], 16)
            sp.wait_ge(gate_ready, 1)
            sp.dma_start(gates_d, gate_b[:, :]).then_inc(gates_stored, 16)
            sp.wait_ge(gates_stored, 16)
            src = gates_d.rearrange("(i b) d -> b i d", b=TB)
            for b in range(TB):
                sp.dma_start(gate[L * b:L * (b + 1), :, :],
                             src[b:b + 1, :, :].broadcast_to([L, NT, 2 * D])).then_inc(gates_in, 16)
            sp.wait_ge(zeros_ready, 3)

            def spread(g, p):
                wait(sp, pv_done, 4 * g - 4)
                wait(sp, s_ready, 4 * g - 4)
                sp.wait_ge(qkv_moved, 3 * g + 2)
                for a in range(HQ):
                    sp.dma_start(Qx[L * a:L * (a + 1), p, :, a, :], by_seq(Qs[L * a:L * (a + 1), p, :])).then_inc(qk_spread[p], 16)
                for a in range(HQ):
                    for q in range(HQ):
                        at = L * a + HD * q
                        sp.dma_start(Kx[at:at + HD, p, q, :], Ks[at:at + HD, p, :]).then_inc(qk_spread[p], 16)
                sp.wait_ge(qkv_moved, 3 * g + 3)
                vs = Vs[:, p, :].rearrange("p (t a w) -> p t a w", t=TG, a=HQ)
                vx = Vx[:, p, :, :, :].rearrange("p (t b) a w -> p b t a w", b=TB)
                for b in range(TB):
                    for a in range(HQ):
                        sp.dma_start(vx[L * a:L * (a + 1), b, :, a, :],
                                     vs[L * b:L * (b + 1), :, a, :]).then_inc(v_spread[p], 16)

            spread(0, 0)
            with sp.Fori(0, 3) as i:
                spread(i * 2 + 1, 1)
                spread(i * 2 + 2, 0)
            spread(7, 1)

            for g in range(NG):
                sp.wait_ge(x_updated, 3 * NG + 1 + g)
                sp.dma_start(ov[:, x_group(g), :], X[:, x_group(g), :]).then_inc(out_done, 16)
            sp.wait_ge(out_done, 16 * NG)

        @block.gpsimd
        def _(pool):
            pool.memset(ident[:, :], 0.0)
            pool.memset(minus_half[:, :], -0.5).then_inc(pool_chain, 1)
            pool.wait_ge(pool_chain, 1)
            pool.affine_select(out=ident[:, :], in_=ident[:, :], compare_op=ALU.not_equal, fill=1.0, base=0,
                               pattern=[[-1, P]], channel_multiplier=1).then_inc(consts_ready, 1)
            pool.memset(Kx[:, :, :, :], 0.0).then_inc(zeros_ready, 1)

            def power(gg, p):
                pool.wait_ge(v_ready, gg + 1)
                wait(pool, xhat_ready, gg - 1)
                pool.tensor_tensor(rstd[:, p, :], v_sb[:, p, :], minus_half[:, :], ALU.pow).then_inc(pool_chain, 1)
                pool.wait_ge(pool_chain, gg + 2)
                pool.tensor_tensor(shift[:, p, :], mk[:, p, :], rstd[:, p, :], ALU.mult).then_inc(rstd_ready, 1)

            def add_shift(gg, p, phase=0, g=-1):
                pool.wait_ge(hA_ready, gg + 1)
                if phase == 0:
                    wait(pool, qkv_ready, 3 * (g + 1))
                elif phase == 2:
                    pool.wait_ge(qkv1_ready, 3 * (g + 1))
                else:
                    pool.wait_ge(u_ready, NC * ((phase // 2) * NG + g + 1))
                pool.tensor_tensor(by_seq(h[:, p, :]), by_seq(hA[:, p, :]),
                                   B[:, seqs(gg)].unsqueeze(2).broadcast_to([P, GB, L]), ALU.add).then_inc(h_ready, 1)

            def keep(phase, g, p):
                gg = phase * NG + g
                bias = r(["bproj0", "b2_0", "bproj1", "b2_1"][phase]).unsqueeze(1).broadcast_to([P, TG, D])
                wait(pool, x_updated, gg - 1)
                if phase < 2:
                    pool.tensor_tensor(by_tile(gb[:, :]), gate[:, x_group(g), D * phase:D * (phase + 1)], bias,
                                       ALU.mult).then_inc(gb_ready, 1)
                    pool.wait_ge(gb_ready, gg + 1)
                    pool.tensor_tensor(by_tile(xg[:, p, :]), by_tile(gb[:, :]), X[:, x_group(g), :],
                                       ALU.add).then_inc(xg_ready, 1)
                else:
                    pool.tensor_tensor(by_tile(xg[:, p, :]), X[:, x_group(g), :], bias, ALU.add).then_inc(xg_ready, 1)

            power(0, 0)
            power(1, 1)
            power(2, 0)
            pool.memset(Vx[:, :, :, :, :], 0.0).then_inc(zeros_ready, 1)
            pool.wait_ge(ab_ready, 1)
            add_shift(0, 0)
            add_shift(1, 1)
            for i in range(5):
                pool.wait_ge(x_in[i], 16)
            pool.wait_ge(gates_in, 16 * TB)
            pool.wait_ge(rows_ready, 1)
            for phase in range(4):
                def step(g, p, phase=phase):
                    gg = phase * NG + g
                    keep(phase, g, p)
                    if phase < 3 or not isinstance(g, int) or g < 6:
                        add_shift(gg + 2, p, phase, g)
                    if phase < 3 or not isinstance(g, int) or g < 5:
                        power(gg + 3, 1 - p)
                group_steps(pool, step, 6 if phase < 3 else 4)

        @block.vector
        def _(dve):
            links = [0]

            def link(ins):
                links[0] += 1
                ins.then_inc(dve_pre, 1)
                dve.wait_ge(dve_pre, links[0])

            dve.memset(kind[:, 0, 0:2 * NG], 0.0)
            dve.memset(kind[:, 0, 2 * NG:], 1.0)
            dve.memset(kind[:, 1, 0:2 * NG], -1.0)
            dve.memset(kind[:, 1, 2 * NG:], 0.0)
            dve.memset(kind[:, 2, 0:2 * NG], 1e-5)
            dve.memset(kind[:, 2, 2 * NG:], 1e-6)
            dve.memset(Vs[:, :, :], 1.0).then_inc(zeros_ready, 1)
            link(dve.memset(Qx[:, :, :, :, :], 0.0))
            dve.sem_inc(zeros_ready, 1)
            link(dve.memset(mask[:, :], OFF_BLOCK))
            for b in range(TB):
                last = dve.memset(mask[L * b:L * (b + 1), L * b:L * (b + 1)], 0.0)
            link(last)

            def row_stats(gg):
                for t in range(TG):
                    last = dve.bn_stats(stats[:, t, :], X[:, x_tile(gg, t), :])
                last.then_inc(stats_done, 1)

            def aggregate(gg, p):
                for t in range(TG):
                    last = dve.bn_aggr(mv[:, t, :], stats[:, t, :])
                last.then_inc(mv_done, 1)
                dve.wait_ge(mv_done, gg + 1)
                wait(dve, rstd_ready, gg - 1)
                dve.scalar_tensor_tensor(out=sqm[:, :], in0=mv[:, :, 0], scalar=kind[:, 0, one(gg)], in1=mv[:, :, 0],
                                         op0=ALU.mult, op1=ALU.mult).then_inc(dve_chain, 1)
                dve.tensor_scalar(mk[:, p, :], mv[:, :, 0], kind[:, 1, one(gg)], None, ALU.mult)
                dve.wait_ge(dve_chain, gg + 1)
                dve.scalar_tensor_tensor(out=v_sb[:, p, :], in0=sqm[:, :], scalar=kind[:, 2, one(gg)], in1=mv[:, :, 1],
                                         op0=ALU.add, op1=ALU.add).then_inc(v_ready, 1)

            def modulate(gg, p, stats_of=None):
                if stats_of is not None:
                    dve.wait_ge(stats_done, stats_of + 1)
                dve.wait_ge(hT_ready, gg + 1)
                wait(dve, h_ready, gg - 1)
                dve.tensor_tensor(by_seq(hA[:, p, :]), by_seq(hT_ps[:, :]),
                                  A[:, seqs(gg)].unsqueeze(2).broadcast_to([P, GB, L]), ALU.mult).then_inc(hA_ready, 1)

            def update(phase, g, p):
                gg = phase * NG + g
                if phase == 2:
                    dve.wait_ge(p1_ready, g + 1)
                    dve.reciprocal(rden1[:, :], den1[:, p, :]).then_inc(rden1_ready, 1)
                    dve.wait_ge(rden1_ready, g + 1)
                dve.wait_ge(y_ready, gg + 1)
                if phase < 2:
                    wait(dve, x_updated, gg)
                    dve.tensor_tensor(by_tile(yG[:, :]), by_tile(y_ps[:, :]), gate[:, x_group(g), D * phase:D * (phase + 1)],
                                      ALU.mult).then_inc(y_used, 1)
                    dve.wait_ge(y_used, gg + 1)
                    dve.wait_ge(xg_ready, gg + 1)
                    dve.tensor_tensor(X[:, x_group(g), :], by_tile(yG[:, :]), by_tile(xg[:, p, :]),
                                      ALU.add).then_inc(x_updated, 1)
                elif phase == 2:
                    dve.wait_ge(xg_ready, gg + 1)
                    for t in range(TG):
                        last = dve.scalar_tensor_tensor(
                            out=X[:, x_tile(g, t), :], in0=y_ps[:, P * t:P * (t + 1)], scalar=rden1[:, t:t + 1],
                            in1=xg[:, p, P * t:P * (t + 1)], op0=ALU.mult, op1=ALU.add)
                    last.then_inc(x_updated, 1)
                else:
                    dve.wait_ge(xg_ready, gg + 1)
                    dve.tensor_tensor(X[:, x_group(g), :], by_tile(y_ps[:, :]), by_tile(xg[:, p, :]),
                                      ALU.add).then_inc(x_updated, 1)

            def scores_max(g, t):
                tile, q = 4 * g + t, t % 2
                S = bank[4 + q][:, :].rearrange("p (n k) -> p n k", k=L)
                dve.wait_ge(s_ready, tile + 1)
                dve.tensor_reduce(smax[:, q, :], S, AX_X, ALU.max).then_inc(smax_ready, 1)
                dve.wait_ge(smax_ready, tile + 1)
                dve.tensor_tensor(Ss[:, q, :].rearrange("p (n k) -> p n k", k=L), S,
                                  smax[:, q, :].unsqueeze(2).broadcast_to([P, TB * HQ, L]),
                                  ALU.subtract).then_inc(s_used, 1)
                dve.wait_ge(s_used, tile + 1)
                wait(dve, pt_ready, tile - 1)
                dve.transpose(St[:, q, :], Ss[:, q, :]).then_inc(st_ready, 1)

            def normalise(g, p, half):
                O = bank[6 + half][:, 0:2 * OW].rearrange("p (n w) -> p n w", w=VW)
                dve.wait_ge(pv_done, 4 * g + 2 * half + 2)
                dve.reciprocal(rden[:, :].unsqueeze(2), O[:, :, HD:VW]).then_inc(rden_ready, 1)
                dve.wait_ge(rden_ready, 2 * g + half + 1)
                wait(dve, ot_ready, g)
                dve.tensor_tensor(On[:, p, 2 * P * half:2 * P * (half + 1)].rearrange("p (n d) -> p n d", d=HD),
                                  O[:, :, 0:HD], rden[:, :].unsqueeze(2).broadcast_to([P, 2 * H, HD]),
                                  ALU.mult).then_inc(o_used, 1)

            def softmax1(g, p):
                dve.wait_ge(s1_ready, g + 1)
                dve.tensor_tensor(by_tile(Ss[:, p, :]), by_tile(bank[7][:, :]),
                                  mask[:, :].unsqueeze(1).broadcast_to([P, TG, P]), ALU.add).then_inc(s1_masked, 1)
                dve.wait_ge(s1_masked, g + 1)
                dve.tensor_reduce(max1[:, :], by_tile(Ss[:, p, :]), AX_X, ALU.max).then_inc(max1_ready, 1)
                dve.wait_ge(max1_ready, g + 1)
                dve.tensor_scalar(nmax1[:, p, :], max1[:, :], -SCALE1, None, ALU.mult).then_inc(sm1_ready, 1)

            for gg in range(3):
                dve.wait_ge(x_in[gg], 16)
                row_stats(gg)
                dve.wait_ge(stats_done, gg + 1)
                aggregate(gg, gg % 2)
            dve.wait_ge(exp_c, 1)
            link(dve.tensor_scalar(s_tok[:, :], e_tok[:, :], 1.0, None, ALU.add))
            link(dve.reciprocal(e_tok[:, :], s_tok[:, :]))
            dve.tensor_tensor(s_tok[:, :], c_tok[:, :], e_tok[:, :], ALU.mult).then_inc(silu_ready, 1)
            dve.wait_ge(condT_ready, 1)
            dve.tensor_copy(cT[:, :], bank[1][:, 0:NB])
            dve.tensor_copy(sT[:, :], bank[1][:, NB:2 * NB]).then_inc(condT_copied, 1)
            dve.wait_ge(col_in, 32)
            for n, (name, i) in enumerate((("bt", 1), ("bt", 4), ("f1b", 0), ("f2b", 0))):
                dve.tensor_scalar(one_plus[:, n:n + 1], c(name, i), 1.0, None, ALU.add)
            dve.tensor_scalar(q_bias[:, :], c("bq"), SCALE0, None, ALU.mult)
            dve.tensor_copy(bcol[:, 0, :], c("bv").broadcast_to([D, D]))
            link(dve.tensor_copy(bcol[:, 1, :], c("v1b").broadcast_to([D, D])))
            dve.wait_ge(film_ready, 1)
            for phase, (g_, be, sh) in enumerate((("g1", "be1", 0), ("g2", "be2", 3))):
                at = slice(phase * NB, (phase + 1) * NB)
                scale_ps = bank[2][:, (2 * phase + 1) * NB:(2 * phase + 2) * NB]
                shift_ps = bank[2][:, 2 * phase * NB:(2 * phase + 1) * NB]
                dve.tensor_scalar(A[:, at], scale_ps, one_plus[:, phase:phase + 1], c(g_), ALU.add, ALU.mult)
                link(dve.tensor_scalar(t_mul[:, :], scale_ps, one_plus[:, phase:phase + 1], c(be), ALU.add, ALU.mult))
                link(dve.scalar_tensor_tensor(out=B[:, at], in0=shift_ps, scalar=c("bt", sh), in1=t_mul[:, :],
                                              op0=ALU.add, op1=ALU.add))
            for phase, (n_, f) in ((2, ("n1", "f1b")), (3, ("n2", "f2b"))):
                at = slice(phase * NB, (phase + 1) * NB)
                scale_ps = bank[3][:, (2 * phase - 4) * NB:(2 * phase - 3) * NB]
                shift_ps = bank[3][:, (2 * phase - 3) * NB:(2 * phase - 2) * NB]
                dve.tensor_scalar(A[:, at], scale_ps, one_plus[:, phase:phase + 1], c(n_), ALU.add, ALU.mult)
                last = dve.tensor_scalar(B[:, at], shift_ps, c(f, 1), None, ALU.add)
            link(last)
            dve.sem_inc(ab_ready, 1)
            modulate(0, 0)
            dve.tensor_tensor(gate_b[:, 0:D], bank[4][:, 0:D], r("gate0"), ALU.add)
            dve.tensor_tensor(gate_b[:, D:2 * D], bank[4][:, D:2 * D], r("gate1"), ALU.add).then_inc(gate_ready, 1)
            modulate(1, 1)
            dve.wait_ge(fold_ready, 1)
            dve.tensor_copy(vT[:, :], bank[5][:, 0:D]).then_inc(fold_copied, 1)
            dve.wait_ge(fold_ready, 2)
            dve.tensor_copy(wvp[:, :], bank[5][:, D:2 * D])
            dve.tensor_tensor(r("bproj0"), bank[5][:, 2 * D:3 * D], r("bproj0"), ALU.add)
            dve.tensor_tensor(r("bproj1"), bank[5][:, 3 * D:4 * D], r("bproj1"), ALU.add).then_inc(rows_ready, 1)
            dve.wait_ge(x_in[3], 16)
            dve.wait_ge(x_in[4], 16)
            dve.wait_ge(gates_in, 16 * TB)

            def attention0(g, p):
                if not (isinstance(g, int) and g == 0):
                    normalise(g - 1, 1 - p, 1)
                scores_max(g, 0)
                scores_max(g, 1)
                row_stats(g + 3)
                modulate(g + 2, p, g + 3)
                aggregate(g + 3, 1 - p)
                scores_max(g, 2)
                if not (isinstance(g, int) and g == 0):
                    update(0, g - 1, 1 - p)
                normalise(g, p, 0)
                scores_max(g, 3)

            def mlp(phase):
                def step(g, p):
                    gg = phase * NG + g
                    if isinstance(g, int) and g == 0:
                        if phase == 1:
                            normalise(7, 1, 1)
                        else:
                            softmax1(7, 1)
                    if phase < 3 or not isinstance(g, int) or g < 5:
                        row_stats(gg + 3)
                        modulate(gg + 2, p, gg + 3)
                        aggregate(gg + 3, 1 - p)
                    elif g < 6:
                        modulate(gg + 2, p)
                    if isinstance(g, int) and g == 0:
                        update(phase - 1, 7, 1)
                    else:
                        update(phase, g - 1, 1 - p)
                return step

            def attention1(g, p):
                if not (isinstance(g, int) and g == 0):
                    softmax1(g - 1, 1 - p)
                row_stats(2 * NG + g + 3)
                modulate(2 * NG + g + 2, p, 2 * NG + g + 3)
                aggregate(2 * NG + g + 3, 1 - p)
                if isinstance(g, int) and g == 0:
                    update(1, 7, 1)
                else:
                    update(2, g - 1, 1 - p)

            group_steps(dve, attention0)
            group_steps(dve, mlp(1))
            group_steps(dve, attention1)
            group_steps(dve, mlp(3), 4)
            update(3, 7, 1)

        @block.scalar
        def _(act):
            act.dma_start(col[:, :], columns).then_inc(col_in, 16)
            act.dma_start(row[:, :, :], rows.unsqueeze(0).broadcast_to([P, len(R_NAMES), D])).then_inc(col_in, 16)
            cut = [0, W_AT["Wproj"][0], W_AT["W1_0"][0], W_ALL]
            for s_in, lo, hi in zip((wt_in, wrest_in, wmlp_in), cut, cut[1:]):
                act.dma_start(W[:, lo:hi], weights[:, lo:hi]).then_inc(s_in, 16)
            act.wait_ge(cond_in, 16)
            act.activation(e_tok[:, :], c_tok[:, :], ACT.Exp, scale=-1.0).then_inc(exp_c, 1)

            def apply(gg, p):
                act.wait_ge(rstd_ready, gg + 1)
                wait(act, hT_ready, gg - 1)
                for t in range(TG):
                    last = act.activation(xhat[:, p, P * t:P * (t + 1)], X[:, x_tile(gg, t), :], ACT.Identity,
                                          bias=shift[:, p, t:t + 1], scale=rstd[:, p, t:t + 1])
                last.then_inc(xhat_ready, 1)

            def move_qk(g, p, k, which):
                act.wait_ge(qkv_ready, 3 * g + which + 1)
                wait(act, qk_spread[p], 16 * QK_DMAS * k)
                if which == 0:
                    act.activation(Qs[:, p, :], bank[2][:, :], ACT.Identity, bias=q_bias[:, :],
                                   scale=SCALE0).then_inc(qkv_moved, 1)
                else:
                    act.activation(Ks[:, p, :], bank[3][:, :], ACT.Identity, bias=c("bk")).then_inc(qkv_moved, 1)

            def move_v(g, p, k):
                act.wait_ge(qkv_ready, 3 * g + 3)
                wait(act, v_spread[p], 16 * V_DMAS * k)
                vs = Vs[:, p, :].rearrange("p (n w) -> p n w", w=VW)
                act.activation(vs[:, :, 0:HD], bank[2][:, :].rearrange("p (n d) -> p n d", d=HD),
                               ACT.Copy).then_inc(qkv_moved, 1)

            def exps(g, t):
                tile = 4 * g + t
                act.wait_ge(st_ready, tile + 1)
                wait(act, pv_done, tile - 3)
                act.activation(PT[:, t, :], St[:, t % 2, :], ACT.Exp).then_inc(pt_ready, 1)

            def move_o(g, p):
                act.wait_ge(ot_ready, g + 1)
                wait(act, y_ready, g)
                act.activation(OTs[:, p, :], bank[1][:, :], ACT.Copy).then_inc(ot_moved, 1)

            def gelus(m, p):
                for n in range(NC):
                    act.wait_ge(u_ready, NC * m + n + 1)
                    bias = c("b1_0" if m_layer[0] == 0 else "b1_1", n)
                    act.activation(gT[:, p, n, :], bank[2 + n][:, :], ACT.Gelu, bias=bias).then_inc(g_ready, 1)

            m_layer = [0]
            apply(0, 0)
            apply(1, 1)
            apply(2, 0)
            act.wait_ge(zeros_ready, 4)
            act.wait_ge(dve_pre, 4)
            act.wait_ge(ab_ready, 1)
            move_qk(0, 0, 0, 0)
            move_qk(0, 0, 0, 1)
            move_v(0, 0, 0)

            def attention0(g, p, k=0):
                more = not (isinstance(g, int) and g == NG - 1)
                if more:
                    move_qk(g + 1, 1 - p, k, 0)
                    move_qk(g + 1, 1 - p, k, 1)
                exps(g, 0)
                if more:
                    move_v(g + 1, 1 - p, k)
                if not (isinstance(g, int) and g == 0):
                    move_o(g - 1, 1 - p)
                exps(g, 1)
                exps(g, 2)
                exps(g, 3)
                apply(g + 3, 1 - p)

            attention0(0, 0, 0)
            with act.Fori(0, 3) as i:
                attention0(i * 2 + 1, 1, i + 1)
                attention0(i * 2 + 2, 0, i + 1)
            attention0(7, 1)

            def mlp(phase):
                def step(g, p):
                    m_layer[0] = phase // 2
                    m = (phase // 2) * NG + g
                    if isinstance(g, int) and g == 0 and phase == 3:
                        exps1(7, 1)
                    gelus(m, p)
                    if isinstance(g, int) and g == 0:
                        if phase == 1:
                            move_o(7, 1)
                        else:
                            move_p1(7, 1)
                    if phase < 3 or not isinstance(g, int) or g < 5:
                        apply(phase * NG + g + 3, 1 - p)
                return step

            def exps1(g, p):
                act.wait_ge(sm1_ready, g + 1)
                wait(act, x_updated, 2 * NG + g - 1)
                for t in range(TG):
                    last = act.activation(St[:, p, P * t:P * (t + 1)], Ss[:, p, P * t:P * (t + 1)], ACT.Exp,
                                          scale=SCALE1, bias=nmax1[:, p, t:t + 1], accum_out=den1[:, p, t:t + 1])
                last.then_inc(p1_ready, 1)

            def move_p1(g, p):
                act.wait_ge(p1T_ready, g + 1)
                act.activation(PT[:, p, :], bank[6][:, :], ACT.Copy).then_inc(p1T_moved, 1)

            def move_qkv1(g, p, which):
                act.wait_ge(qkv1_ready, 3 * g + which + 1)
                if which == 0:
                    act.activation(Qs[:, p, :], bank[2][:, :], ACT.Identity, bias=c("q1b")).then_inc(qkv1_moved, 1)
                elif which == 1:
                    act.activation(Ks[:, p, :], bank[3][:, :], ACT.Identity, bias=c("k1b")).then_inc(qkv1_moved, 1)
                else:
                    act.activation(Vs[:, p, 0:GN], bank[4][:, :], ACT.Copy).then_inc(qkv1_moved, 1)

            def attention1(g, p):
                first = isinstance(g, int) and g == 0
                if not first:
                    exps1(g - 1, 1 - p)
                move_qkv1(g, p, 0)
                if not first:
                    move_p1(g - 1, 1 - p)
                move_qkv1(g, p, 1)
                move_qkv1(g, p, 2)
                apply(2 * NG + g + 3, 1 - p)

            group_steps(act, mlp(1))
            group_steps(act, attention1)
            group_steps(act, mlp(3), 4)

        @block.tensor
        def _(pe):
            pe.wait_ge(consts_ready, 1)
            pe.wait_ge(silu_ready, 1)
            pe.transpose(bank[1][:, 0:NB], c_tok[:, :], ident[:, :])
            pe.transpose(bank[1][:, NB:2 * NB], s_tok[:, :], ident[:, :]).then_inc(condT_ready, 1)

            def rows_T(gg, p):
                pe.wait_ge(xhat_ready, gg + 1)
                wait(pe, hA_ready, gg)
                for t in range(TG):
                    last = pe.transpose(hT_ps[:, P * t:P * (t + 1)], xhat[:, p, P * t:P * (t + 1)], ident[:, :])
                last.then_inc(hT_ready, 1)

            rows_T(0, 0)
            pe.wait_ge(condT_copied, 1)
            pe.wait_ge(wt_in, 16)
            for n, i in enumerate((0, 1, 3, 4)):
                pe.matmul(bank[2][:, n * NB:(n + 1) * NB], w("Wt", i), sT[:, :], start=True, stop=True)
            for n, name in enumerate(("film1", "film2")):
                for i in range(2):
                    pe.matmul(bank[3][:, (2 * n + i) * NB:(2 * n + i + 1) * NB], w(name, i), cT[:, :], start=True, stop=True)
            for n, i in enumerate((2, 5)):
                last = pe.matmul(bank[4][:, n * D:(n + 1) * D], sT[:, :], w("Wt", i), start=True, stop=True)
            last.then_inc(film_ready, 1)
            pe.wait_ge(wrest_in, 16)
            rows_T(1, 1)
            pe.transpose(bank[5][:, 0:D], w("v1"), ident[:, :]).then_inc(fold_ready, 1)

            def qkv0(g, p):
                pe.wait_ge(h_ready, g + 1)
                wait(pe, qkv_moved, 3 * g)
                pe.matmul(bank[2][:, :], w("Wqkv", 0), h[:, p, :], start=True, stop=True).then_inc(qkv_ready, 1)
                pe.matmul(bank[3][:, :], w("Wqkv", 1), h[:, p, :], start=True, stop=True).then_inc(qkv_ready, 1)
                pe.wait_ge(qkv_moved, 3 * g + 1)
                for t in range(TG):
                    last = pe.matmul(bank[2][:, P * t:P * (t + 1)], h[:, p, P * t:P * (t + 1)], w("Wqkv", 2),
                                     start=True, stop=True)
                last.then_inc(qkv_ready, 1)

            def scores0(g, p, t):
                tile = 4 * g + t
                wait(pe, s_used, tile - 1)
                for b in range(TB):
                    at = P * t + L * b
                    last = pe.matmul(bank[4 + t % 2][:, P * b:P * (b + 1)], Qx[:, p, TB * t + b, :, :].rearrange("p a t -> p (a t)"), Kx[:, p, :, at:at + L],
                                     start=True, stop=True)
                last.then_inc(s_ready, 1)

            def values0(g, p, t):
                tile = 4 * g + t
                pe.wait_ge(pt_ready, tile + 1)
                if t % 2 == 0:
                    wait(pe, o_used, 2 * g - 1 + t // 2)
                for q in range(HQ):
                    for b in range(TB):
                        at = (t % 2) * OW + q * HQ * VW
                        last = pe.matmul(bank[6 + t // 2][L * b:L * (b + 1), at:at + HQ * VW],
                                         PT[:, t, P * b + L * q:P * b + L * (q + 1)],
                                         Vx[:, p, TB * t + b, :, VW * q:VW * (q + 1)], start=True, stop=True)
                last.then_inc(pv_done, 1)

            def output_T(g, p):
                pe.wait_ge(o_used, 2 * g + 2)
                wait(pe, y_used, g)
                for t in range(TG):
                    last = pe.transpose(bank[1][:, P * t:P * (t + 1)], On[:, p, P * t:P * (t + 1)], ident[:, :])
                last.then_inc(ot_ready, 1)

            def project0(g, p):
                pe.wait_ge(ot_moved, g + 1)
                for t in range(TG):
                    last = pe.matmul(y_ps[:, P * t:P * (t + 1)], OTs[:, p, P * t:P * (t + 1)], w("Wproj"),
                                     start=True, stop=True)
                last.then_inc(y_ready, 1)

            qkv0(0, 0)
            pe.wait_ge(fold_copied, 1)
            pe.matmul(bank[5][:, D:2 * D], vT[:, :], w("proj1"), start=True, stop=True)
            pe.matmul(bank[5][:, 2 * D:3 * D], bcol[:, 0, :], w("Wproj"), start=True, stop=True)
            pe.matmul(bank[5][:, 3 * D:4 * D], bcol[:, 1, :], w("proj1"), start=True, stop=True).then_inc(fold_ready, 1)
            pe.wait_ge(rows_ready, 1)

            def attention0(g, p, k=None):
                first = isinstance(g, int) and g == 0
                if not (isinstance(g, int) and g == NG - 1):
                    qkv0(g + 1, 1 - p)
                pe.wait_ge(qk_spread[p], 16 * QK_DMAS * (k + 1))
                scores0(g, p, 0)
                if not first:
                    output_T(g - 1, 1 - p)
                scores0(g, p, 1)
                pe.wait_ge(v_spread[p], 16 * V_DMAS * (k + 1))
                values0(g, p, 0)
                rows_T(g + 2, p)
                scores0(g, p, 2)
                if not first:
                    project0(g - 1, 1 - p)
                values0(g, p, 1)
                scores0(g, p, 3)
                values0(g, p, 2)
                values0(g, p, 3)

            attention0(0, 0, 0)
            with pe.Fori(0, 3) as i:
                attention0(i * 2 + 1, 1, i)
                attention0(i * 2 + 2, 0, i + 1)
            attention0(7, 1, 3)

            def up(phase, g, p):
                m = (phase // 2) * NG + g
                pe.wait_ge(h_ready, phase * NG + g + 1)
                for n in range(NC):
                    wait(pe, g_ready, NC * (m - 1) + n + 1)
                    last = pe.matmul(bank[2 + n][:, :], w(f"W1_{phase // 2}", n), h[:, p, :], start=True, stop=True)
                    last.then_inc(u_ready, 1)

            def down(phase, g, p):
                gg, m = phase * NG + g, (phase // 2) * NG + g
                pe.wait_ge(g_ready, NC * (m + 1))
                pe.wait_ge(y_used if phase == 1 else x_updated, gg)
                for t in range(TG):
                    for n in range(NC):
                        last = pe.matmul(y_ps[:, P * t:P * (t + 1)], gT[:, p, n, P * t:P * (t + 1)],
                                         w(f"W2_{phase // 2}", n), start=(n == 0), stop=(n == NC - 1))
                last.then_inc(y_ready, 1)

            def qkv1(g, p):
                pe.wait_ge(h_ready, 2 * NG + g + 1)
                wait(pe, qkv1_moved, 3 * g)
                pe.matmul(bank[2][:, :], w("q1"), h[:, p, :], start=True, stop=True).then_inc(qkv1_ready, 1)
                pe.matmul(bank[3][:, :], w("k1"), h[:, p, :], start=True, stop=True).then_inc(qkv1_ready, 1)
                for t in range(TG):
                    last = pe.matmul(bank[4][:, P * t:P * (t + 1)], h[:, p, P * t:P * (t + 1)], wvp[:, :],
                                     start=True, stop=True)
                last.then_inc(qkv1_ready, 1)

            def scores1(g, p):
                pe.wait_ge(qkv1_moved, 3 * g + 3)
                wait(pe, s1_masked, g)
                for t in range(TG):
                    at = slice(P * t, P * (t + 1))
                    last = pe.matmul(bank[7][:, at], Qs[:, p, at], Ks[:, p, at], start=True, stop=True)
                last.then_inc(s1_ready, 1)

            def probs_T(g, p):
                pe.wait_ge(p1_ready, g + 1)
                wait(pe, p1T_moved, g)
                for t in range(TG):
                    last = pe.transpose(bank[6][:, P * t:P * (t + 1)], St[:, p, P * t:P * (t + 1)], ident[:, :])
                last.then_inc(p1T_ready, 1)

            def values1(g, p):
                pe.wait_ge(p1T_moved, g + 1)
                pe.wait_ge(x_updated, 2 * NG + g)
                for t in range(TG):
                    at = slice(P * t, P * (t + 1))
                    last = pe.matmul(y_ps[:, at], PT[:, p, at], Vs[:, p, at], start=True, stop=True)
                last.then_inc(y_ready, 1)

            def mlp(phase):
                def step(g, p):
                    gg = phase * NG + g
                    first = isinstance(g, int) and g == 0
                    if first and phase == 3:
                        scores1(7, 1)
                    up(phase, g, p)
                    if first and phase == 1:
                        output_T(7, 1)
                    if first and phase == 3:
                        probs_T(7, 1)
                    if phase < 3 or not isinstance(g, int) or g < 6:
                        rows_T(gg + 2, p)
                    if not first:
                        down(phase, g - 1, 1 - p)
                    elif phase == 1:
                        project0(7, 1)
                    else:
                        values1(7, 1)
                return step

            def attention1(g, p):
                first = isinstance(g, int) and g == 0
                if first:
                    rows_T(2 * NG + g + 2, p)
                    down(1, 7, 1)
                    qkv1(0, 0)
                else:
                    scores1(g - 1, 1 - p)
                    qkv1(g, p)
                    probs_T(g - 1, 1 - p)
                    rows_T(2 * NG + g + 2, p)
                    values1(g - 1, 1 - p)

            pe.wait_ge(s_used, 4 * NG)
            pe.wait_ge(wmlp_in, 16)
            group_steps(pe, mlp(1))
            group_steps(pe, attention1)
            group_steps(pe, mlp(3), 4)
            down(3, 7, 1)


def kernel(x, cond_1024, L0_cond_Wqkv, L0_cond_bqkv, L0_cond_Wproj, L0_cond_bproj, L0_cond_W1, L0_cond_b1,
           L0_cond_W2, L0_cond_b2, L0_cond_Wt, L0_cond_bt, L0_cond_g1, L0_cond_be1, L0_cond_g2, L0_cond_be2,
           L1_cond_norm1_w, L1_cond_film1_w, L1_cond_film1_b, L1_cond_q_w, L1_cond_q_b, L1_cond_k_w, L1_cond_k_b,
           L1_cond_v_w, L1_cond_v_b, L1_cond_proj_w, L1_cond_proj_b, L1_cond_norm2_w, L1_cond_film2_w,
           L1_cond_film2_b, L1_cond_mlp_w1, L1_cond_mlp_b1, L1_cond_mlp_w2, L1_cond_mlp_b2):
    import numpy as np
    import concourse.bacc as bacc
    from concourse.bass_utils import run_bass_kernel_spmd

    def by_a(m):
        return m.reshape(m.shape[:-1] + (HQ, HQ, HD)).swapaxes(-3, -2).reshape(m.shape)

    def chunks(m):
        return m.reshape(-1, P, m.shape[-1]).swapaxes(0, 1).reshape(P, -1)

    wqkv = np.asarray(L0_cond_Wqkv).reshape(D, 3, D)
    bqkv = np.asarray(L0_cond_bqkv).reshape(3, D)
    bt = np.asarray(L0_cond_bt).reshape(6, D)
    ws = {"Wt": L0_cond_Wt, "film1": L1_cond_film1_w, "film2": L1_cond_film2_w, "Wproj": L0_cond_Wproj,
          "v1": L1_cond_v_w, "proj1": L1_cond_proj_w, "Wqkv": by_a(wqkv).reshape(D, 3 * D), "W1_0": L0_cond_W1,
          "W2_0": chunks(np.asarray(L0_cond_W2)), "q1": L1_cond_q_w, "k1": L1_cond_k_w, "W1_1": L1_cond_mlp_w1,
          "W2_1": chunks(np.asarray(L1_cond_mlp_w2))}
    cs = {"bt": bt, "g1": L0_cond_g1, "be1": L0_cond_be1, "g2": L0_cond_g2, "be2": L0_cond_be2, "bq": by_a(bqkv[0]),
          "bk": by_a(bqkv[1]), "bv": bqkv[2], "b1_0": L0_cond_b1, "n1": L1_cond_norm1_w, "n2": L1_cond_norm2_w,
          "f1b": L1_cond_film1_b, "f2b": L1_cond_film2_b, "q1b": L1_cond_q_b, "k1b": L1_cond_k_b, "v1b": L1_cond_v_b,
          "b1_1": L1_cond_mlp_b1}
    rs = {"gate0": bt[2], "gate1": bt[5], "bproj0": L0_cond_bproj, "b2_0": L0_cond_b2, "bproj1": L1_cond_proj_b,
          "b2_1": L1_cond_mlp_b2}
    arrays = {
        "x": np.ascontiguousarray(np.asarray(x).reshape(NB * L, D)),
        "cond": np.ascontiguousarray(np.asarray(cond_1024)),
        "weights": np.ascontiguousarray(np.concatenate([np.asarray(ws[n]) for n, _ in W_NAMES], axis=1)),
        "columns": np.ascontiguousarray(np.concatenate([np.asarray(cs[n]).reshape(-1, D) for n, _ in C_NAMES], axis=0).T),
        "rows": np.ascontiguousarray(np.stack([np.asarray(rs[n]) for n in R_NAMES])),
    }
    nc = bacc.Bacc("TRN2", target_bir_lowering=False, num_devices=1)
    aps = [nc.dram_tensor(n, a.shape, mybir.dt.from_np(a.dtype), kind="ExternalInput").ap() for n, a in arrays.items()]
    out = nc.dram_tensor("out", (NB * L, D), F32, kind="ExternalOutput").ap()
    build(nc, *aps, out)
    result = run_bass_kernel_spmd(nc, [arrays], core_ids=[0])
    return result.results[0]["out"].reshape(NB, L, D)
```

```python
from contextlib import ExitStack

import concourse.bass as bass
from concourse import mybir

F32 = mybir.dt.float32
ALU = mybir.AluOpType
ACT = mybir.ActivationFunctionType
AX_X = mybir.AxisListType.X

P = 128
D = 128
NB = 128
L = 32
H, HD = 16, 8
FF = 512
NC = FF // P
TB = P // L
NT = NB * L // P
TG = 4
NG = NT // TG
GB = TG * TB
GN = TG * P
HQ = 4
VW = HD + 1
OW = H * VW
SCALE0 = HD ** -0.5
SCALE1 = D ** -0.5
OFF_BLOCK = -1.0e30

W_NAMES = [("Wt", 6 * D), ("film1", 2 * D), ("film2", 2 * D), ("Wproj", D), ("v1", D), ("proj1", D),
           ("Wqkv", 3 * D), ("W1_0", FF), ("W2_0", FF), ("q1", D), ("k1", D), ("W1_1", FF), ("W2_1", FF)]
W_AT, W_ALL = {}, 0
for _name, _n in W_NAMES:
    W_AT[_name] = (W_ALL, _n)
    W_ALL += _n
C_NAMES = [("bt", 6), ("g1", 1), ("be1", 1), ("g2", 1), ("be2", 1), ("bq", 1), ("bk", 1), ("bv", 1), ("b1_0", NC),
           ("n1", 1), ("n2", 1), ("f1b", 2), ("f2b", 2), ("q1b", 1), ("k1b", 1), ("v1b", 1), ("b1_1", NC)]
C_AT, C_ALL = {}, 0
for _name, _n in C_NAMES:
    C_AT[_name] = (C_ALL, _n)
    C_ALL += _n
R_NAMES = ["gate0", "gate1", "bproj0", "b2_0", "bproj1", "b2_1"]


def build(nc, x, cond, weights, columns, rows, out):
    with ExitStack() as ctx:
        def sb(name, shape):
            return ctx.enter_context(nc.sbuf_tensor(name, shape, F32))

        def sem(name):
            return ctx.enter_context(nc.semaphore(name))

        gates_d = nc.dram_tensor("gates_scratch", [NB, 2 * D], F32, kind="Internal").ap()
        values_d = nc.dram_tensor("values_scratch", [2, GN, OW], F32, kind="Internal").ap()

        X = sb("X", [P, NT, D])
        gate = sb("gate", [P, NT, 2 * D])
        W = sb("W", [P, W_ALL])
        col = sb("col", [P, C_ALL])
        row = sb("row", [P, len(R_NAMES), D])
        c_tok, e_tok, s_tok = sb("c_tok", [NB, D]), sb("e_tok", [NB, D]), sb("s_tok", [NB, D])
        cT, sT = sb("cT", [D, NB]), sb("sT", [D, NB])
        A, B = sb("A", [D, 4 * NB]), sb("B", [D, 4 * NB])
        t_mul, one_plus = sb("t_mul", [D, NB]), sb("one_plus", [D, 8])
        gate_b = sb("gate_b", [NB, 2 * D])
        vT, wvp, bcol = sb("vT", [D, D]), sb("wvp", [D, D]), sb("bcol", [D, 2, D])
        q_bias, k_bias, r_sums, r_mask = sb("q_bias", [D, 1]), sb("k_bias", [D, HQ]), sb("r_sums", [D, H]), sb("r_mask", [D, HQ])
        ident, mask, minus_half = (
            sb("ident", [P, P]), sb("mask", [P, P]), sb("minus_half", [P, TG]))
        kind = sb("kind", [P, 3, 4 * NG])
        stats, mv = sb("stats", [P, TG, 6]), sb("mv", [P, TG, 2])
        v_sb, mk, rstd, shift = (sb(n, [P, 2, TG]) for n in ("v_sb", "mk", "rstd", "shift"))
        sqm = sb("sqm", [P, TG])
        xhat = sb("xhat", [P, 2, GN])
        hA, h = sb("hA", [P, 2, GN]), sb("h", [P, 2, GN])
        Qs = sb("Qs", [P, 2, GN])
        Vs = sb("Vs", [P, 2, TG * OW])
        Qx = sb("Qx", [P, 2, GB, HQ, L])
        Kx = sb("Kx", [P, 2, HQ, GN])
        Vx = sb("Vx", [P, 2, GB, HQ, HQ * VW])
        smax = sb("smax", [P, 2, TB * HQ])
        Ss, St = sb("Ss", [P, 2, GN]), sb("St", [P, 2, GN])
        PT = sb("PT", [P, TG, GN])
        rden, On, OTs = sb("rden", [P, 2 * H]), sb("On", [P, 2, GN]), sb("OTs", [P, 2, GN])
        xg, yG, gb = sb("xg", [P, GN]), sb("yG", [P, GN]), sb("gb", [P, GN])
        max1, nmax1 = sb("max1", [P, TG]), sb("nmax1", [P, 2, TG])
        den1, rden1 = sb("den1", [P, 2, TG]), sb("rden1", [P, TG])
        gT = Qx[:, :, :, :, :].rearrange("p v (n b) a t -> p v n (b a t)", n=NC)

        bank = [ctx.enter_context(nc.psum_tensor(f"bank{i}", [P, 512], F32)) for i in range(8)]
        hT_ps, y_ps = bank[0], bank[1]

        x_in = [sem(f"x_in{i}") for i in range(5)]
        cond_in, col_in, wt_in, wrest_in, wmlp_in = (sem(n) for n in ("cond_in", "col_in", "wt_in", "wrest_in", "wmlp_in"))
        consts_ready, zeros_ready = sem("consts_ready"), sem("zeros_ready")
        exp_c, silu_ready, dve_pre = sem("exp_c"), sem("silu_ready"), sem("dve_pre")
        condT_ready = sem("condT_ready")
        film_ready, gate_ready, ab_ready = sem("film_ready"), sem("gate_ready"), sem("ab_ready")
        gates_stored, gates_in = sem("gates_stored"), sem("gates_in")
        fold_ready, fold_copied, rows_ready = sem("fold_ready"), sem("fold_copied"), sem("rows_ready")
        stats_done, mv_done, v_ready, rstd_ready = sem("stats_done"), sem("mv_done"), sem("v_ready"), sem("rstd_ready")
        pool_chain, dve_chain = sem("pool_chain"), sem("dve_chain")
        xhat_ready, hT_ready, hA_ready, h_ready = (
            sem(n) for n in ("xhat_ready", "hT_ready", "hA_ready", "h_ready"))
        gb_ready, xg_ready, y_ready, y_used, x_updated = (
            sem(n) for n in ("gb_ready", "xg_ready", "y_ready", "y_used", "x_updated"))
        qkv_ready, qkv_moved, kx_ready = sem("qkv_ready"), sem("qkv_moved"), sem("kx_ready")
        q_spread = [sem(f"q_spread{i}") for i in range(2)]
        v_stored = [sem(f"v_stored{i}") for i in range(2)]
        v_spread = [sem(f"v_spread{i}") for i in range(2)]
        s_ready, smax_ready, s_used, st_ready, pt_ready, pv_done = (
            sem(n) for n in ("s_ready", "smax_ready", "s_used", "st_ready", "pt_ready", "pv_done"))
        rden_ready, o_used, ot_ready, ot_moved = (sem(n) for n in ("rden_ready", "o_used", "ot_ready", "ot_moved"))
        qkv1_ready, qkv1_moved, s1_ready, s1_masked, max1_ready, sm1_ready, p1_ready, p1T_ready, p1T_moved, rden1_ready = (
            sem(n) for n in ("qkv1_ready", "qkv1_moved", "s1_ready", "s1_masked", "max1_ready", "sm1_ready", "p1_ready", "p1T_ready",
                             "p1T_moved", "rden1_ready"))
        u_ready, g_ready = sem("u_ready"), sem("g_ready")
        out_done = sem("out_done")


        def w(name, i=0, n=D):
            at = W_AT[name][0] + i * n
            return W[:, at:at + n]

        def c(name, i=0):
            at = C_AT[name][0] + i
            return col[:, at:at + 1]

        def r(name):
            return row[:, R_NAMES.index(name), :]

        def by_tile(ap):
            return ap.rearrange("p (t d) -> p t d", t=TG)

        def by_seq(ap):
            return ap.rearrange("p (b t) -> p b t", t=L)

        def wait(eng, s, n):
            if not isinstance(n, int) or n > 0:
                eng.wait_ge(s, n)

        def group_steps(eng, step, last_loop=6):
            step(0, 0)
            with eng.Fori(0, last_loop // 2) as i:
                step(i * 2 + 1, 1)
                step(i * 2 + 2, 0)
            for g in range(last_loop + 1, NG):
                step(g, g % 2)

        def x_group(gg):
            if isinstance(gg, int):
                g = gg % NG
                return slice(g * TG, (g + 1) * TG)
            return bass.ds(((gg) % NG) * TG, TG)

        def x_tile(gg, t):
            if isinstance(gg, int):
                return slice((gg % NG) * TG + t, (gg % NG) * TG + t + 1)
            return bass.ds((gg % NG) * TG + t, 1)

        def seqs(gg):
            if isinstance(gg, int):
                return slice(gg * GB, (gg + 1) * GB)
            return bass.ds(gg * GB, GB)

        def one(gg):
            return slice(gg, gg + 1) if isinstance(gg, int) else bass.ds(gg, 1)

        block = ctx.enter_context(nc.Block())

        @block.sync
        def _(sp):
            xv = x.rearrange("(i p) d -> p i d", p=P)
            ov = out.rearrange("(i p) d -> p i d", p=P)
            sp.dma_start(c_tok[:, :], cond).then_inc(cond_in, 16)
            for g in range(4):
                sp.dma_start(X[:, TG * g:TG * (g + 1), :], xv[:, TG * g:TG * (g + 1), :]).then_inc(x_in[g], 16)
            sp.dma_start(X[:, 4 * TG:, :], xv[:, 4 * TG:, :]).then_inc(x_in[4], 16)
            sp.wait_ge(gate_ready, 1)
            sp.dma_start(gates_d, gate_b[:, :]).then_inc(gates_stored, 16)
            sp.wait_ge(gates_stored, 16)
            src = gates_d.rearrange("(i b) d -> b i d", b=TB)
            for b in range(TB):
                sp.dma_start(gate[L * b:L * (b + 1), :, :],
                             src[b:b + 1, :, :].broadcast_to([L, NT, 2 * D])).then_inc(gates_in, 16)
            sp.wait_ge(zeros_ready, 1)

            def spread(g, p, k):
                wait(sp, s_ready, 4 * g - 3)
                sp.wait_ge(qkv_moved, 2 * g + 1)
                for a in range(HQ):
                    sp.dma_start(Qx[L * a:L * (a + 1), p, :, a, :], by_seq(Qs[L * a:L * (a + 1), p, :])).then_inc(q_spread[p], 16)
                sp.wait_ge(qkv_moved, 2 * g + 2)
                wait(sp, pv_done, 4 * g - 3)
                sp.dma_start(values_d[p].rearrange("(t x) w -> x t w", x=P),
                             Vs[:, p, :].rearrange("p (t w) -> p t w", t=TG)).then_inc(v_stored[p], 16)
                sp.wait_ge(v_stored[p], 16 * (k + 1))
                src = values_d[p].rearrange("(b l) (a w) -> a l b w", l=L, a=HQ)
                for a in range(HQ):
                    sp.dma_start(Vx[L * a:L * (a + 1), p, :, a, :], src[a]).then_inc(v_spread[p], 16)

            spread(0, 0, 0)
            with sp.Fori(0, 3) as i:
                spread(i * 2 + 1, 1, i)
                spread(i * 2 + 2, 0, i + 1)
            spread(7, 1, 3)

            for g in range(NG):
                sp.wait_ge(x_updated, 3 * NG + 2 + g)
                sp.dma_start(ov[:, x_group(g), :], X[:, x_group(g), :]).then_inc(out_done, 16)
            sp.wait_ge(out_done, 16 * NG)

        @block.gpsimd
        def _(pool):
            pool.memset(ident[:, :], 0.0)
            pool.memset(minus_half[:, :], -0.5).then_inc(pool_chain, 1)
            pool.wait_ge(pool_chain, 1)
            pool.affine_select(out=ident[:, :], in_=ident[:, :], compare_op=ALU.not_equal, fill=1.0, base=0,
                               pattern=[[-1, P]], channel_multiplier=1).then_inc(consts_ready, 1)

            def power(gg, p):
                pool.wait_ge(v_ready, gg + 1)
                wait(pool, xhat_ready, gg - 1)
                pool.tensor_tensor(rstd[:, p, :], v_sb[:, p, :], minus_half[:, :], ALU.pow).then_inc(pool_chain, 1)
                pool.wait_ge(pool_chain, gg + 2)
                pool.tensor_tensor(shift[:, p, :], mk[:, p, :], rstd[:, p, :], ALU.mult).then_inc(rstd_ready, 1)

            def add_shift(gg, p, phase=0, g=-1):
                pool.wait_ge(hA_ready, gg + 1)
                if phase == 0:
                    wait(pool, qkv_ready, 3 * (g + 1))
                elif phase == 2:
                    pool.wait_ge(qkv1_ready, 3 * (g + 1))
                else:
                    pool.wait_ge(u_ready, NC * ((phase // 2) * NG + g + 1))
                pool.tensor_tensor(by_seq(h[:, p, :]), by_seq(hA[:, p, :]),
                                   B[:, seqs(gg)].unsqueeze(2).broadcast_to([P, GB, L]), ALU.add).then_inc(h_ready, 1)

            def keep(phase, g):
                gg = phase * NG + g
                bias = r(["bproj0", "b2_0", "bproj1", "b2_1"][phase]).unsqueeze(1).broadcast_to([P, TG, D])
                pool.wait_ge(x_updated, gg + 1)
                if phase < 2:
                    pool.tensor_tensor(by_tile(gb[:, :]), gate[:, x_group(g), D * phase:D * (phase + 1)], bias,
                                       ALU.mult).then_inc(gb_ready, 1)
                    pool.wait_ge(gb_ready, gg + 1)
                    pool.tensor_tensor(by_tile(xg[:, :]), by_tile(gb[:, :]), X[:, x_group(g), :],
                                       ALU.add).then_inc(xg_ready, 1)
                else:
                    pool.tensor_tensor(by_tile(xg[:, :]), X[:, x_group(g), :], bias, ALU.add).then_inc(xg_ready, 1)

            def add_gated(phase, g):
                gg = phase * NG + g
                pool.wait_ge(y_used, gg + 2)
                at = x_group(g) if isinstance(g, int) else bass.ds((gg + NG) % NG * TG, TG)
                pool.tensor_tensor(X[:, at, :], by_tile(yG[:, :]), by_tile(xg[:, :]), ALU.add).then_inc(x_updated, 1)

            power(0, 0)
            power(1, 1)
            power(2, 0)
            pool.memset(Qx[:, :, :, :, :], 0.0)
            pool.memset(Vx[:, :, :, :, :], 0.0).then_inc(zeros_ready, 1)
            pool.memset(yG[:, :], 0.0).then_inc(x_updated, 1)
            pool.wait_ge(ab_ready, 1)
            add_shift(0, 0)
            add_shift(1, 1)
            for phase in range(4):
                def step(g, p, phase=phase):
                    gg = phase * NG + g
                    g_first = isinstance(g, int) and g == 0
                    if phase < 3 or not isinstance(g, int) or g < 6:
                        add_shift(gg + 2, p, phase, g)
                    if phase < 3 or not isinstance(g, int) or g < 5:
                        power(gg + 3, 1 - p)
                    if phase == 0 and isinstance(g, int) and g == 0:
                        for i in range(5):
                            pool.wait_ge(x_in[i], 16)
                        pool.wait_ge(gates_in, 16 * TB)
                        pool.wait_ge(rows_ready, 1)
                    if g_first and phase in (1, 2):
                        add_gated(phase - 1, 7)
                    elif phase < 2 and not g_first:
                        add_gated(phase, g - 1)
                    keep(phase, g)
                group_steps(pool, step, 6 if phase < 3 else 4)

        @block.vector
        def _(dve):
            links = [0]

            def link(ins):
                links[0] += 1
                ins.then_inc(dve_pre, 1)
                dve.wait_ge(dve_pre, links[0])

            dve.memset(kind[:, 0, 0:2 * NG], 0.0)
            dve.memset(kind[:, 0, 2 * NG:], 1.0)
            dve.memset(kind[:, 1, 0:2 * NG], -1.0)
            dve.memset(kind[:, 1, 2 * NG:], 0.0)
            dve.memset(kind[:, 2, 0:2 * NG], 1e-5)
            dve.memset(kind[:, 2, 2 * NG:], 1e-6)
            dve.memset(Vs[:, :, :], 1.0)
            link(dve.memset(mask[:, :], OFF_BLOCK))
            for b in range(TB):
                last = dve.memset(mask[L * b:L * (b + 1), L * b:L * (b + 1)], 0.0)
            link(last)

            def row_stats(gg):
                for t in range(TG):
                    last = dve.bn_stats(stats[:, t, :], X[:, x_tile(gg, t), :])
                last.then_inc(stats_done, 1)

            def aggregate(gg, p):
                for t in range(TG):
                    last = dve.bn_aggr(mv[:, t, :], stats[:, t, :])
                last.then_inc(mv_done, 1)
                dve.wait_ge(mv_done, gg + 1)
                wait(dve, rstd_ready, gg - 1)
                dve.scalar_tensor_tensor(out=sqm[:, :], in0=mv[:, :, 0], scalar=kind[:, 0, one(gg)], in1=mv[:, :, 0],
                                         op0=ALU.mult, op1=ALU.mult).then_inc(dve_chain, 1)
                dve.tensor_scalar(mk[:, p, :], mv[:, :, 0], kind[:, 1, one(gg)], None, ALU.mult)
                dve.wait_ge(dve_chain, gg + 1)
                dve.scalar_tensor_tensor(out=v_sb[:, p, :], in0=sqm[:, :], scalar=kind[:, 2, one(gg)], in1=mv[:, :, 1],
                                         op0=ALU.add, op1=ALU.add).then_inc(v_ready, 1)

            def modulate(gg, p, stats_of=None):
                if stats_of is not None:
                    dve.wait_ge(stats_done, stats_of + 1)
                dve.wait_ge(hT_ready, gg + 1)
                wait(dve, h_ready, gg - 1)
                dve.tensor_tensor(by_seq(hA[:, p, :]), by_seq(hT_ps[:, :]),
                                  A[:, seqs(gg)].unsqueeze(2).broadcast_to([P, GB, L]), ALU.mult).then_inc(hA_ready, 1)

            def update(phase, g, p):
                gg = phase * NG + g
                if phase == 2:
                    dve.wait_ge(p1_ready, g + 1)
                    dve.reciprocal(rden1[:, :], den1[:, p, :]).then_inc(rden1_ready, 1)
                    dve.wait_ge(rden1_ready, g + 1)
                dve.wait_ge(y_ready, gg + 1)
                if phase < 2:
                    dve.wait_ge(x_updated, gg + 1)
                    dve.tensor_tensor(by_tile(yG[:, :]), by_tile(y_ps[:, :]), gate[:, x_group(g), D * phase:D * (phase + 1)],
                                      ALU.mult).then_inc(y_used, 1)
                elif phase == 2:
                    dve.wait_ge(xg_ready, gg + 1)
                    for t in range(TG):
                        last = dve.scalar_tensor_tensor(
                            out=X[:, x_tile(g, t), :], in0=y_ps[:, P * t:P * (t + 1)], scalar=rden1[:, t:t + 1],
                            in1=xg[:, P * t:P * (t + 1)], op0=ALU.mult, op1=ALU.add)
                    last.then_inc(x_updated, 1)
                else:
                    dve.wait_ge(xg_ready, gg + 1)
                    dve.tensor_tensor(X[:, x_group(g), :], by_tile(y_ps[:, :]), by_tile(xg[:, :]),
                                      ALU.add).then_inc(x_updated, 1)

            def scores_max(g, t):
                tile, q = 4 * g + t, t % 2
                S = bank[4 + q][:, :].rearrange("p (n k) -> p n k", k=L)
                dve.wait_ge(s_ready, tile + 1)
                dve.tensor_reduce(smax[:, q, :], S, AX_X, ALU.max).then_inc(smax_ready, 1)
                dve.wait_ge(smax_ready, tile + 1)
                dve.tensor_tensor(Ss[:, q, :].rearrange("p (n k) -> p n k", k=L), S,
                                  smax[:, q, :].unsqueeze(2).broadcast_to([P, TB * HQ, L]),
                                  ALU.subtract).then_inc(s_used, 1)
                dve.wait_ge(s_used, tile + 1)
                wait(dve, pt_ready, tile - 1)
                dve.transpose(St[:, q, :], Ss[:, q, :]).then_inc(st_ready, 1)

            def normalise(g, p, half):
                O = bank[6 + half][:, 0:2 * OW].rearrange("p (n w) -> p n w", w=VW)
                dve.wait_ge(pv_done, 4 * g + 2 * half + 2)
                dve.reciprocal(rden[:, :].unsqueeze(2), O[:, :, HD:VW]).then_inc(rden_ready, 1)
                dve.wait_ge(rden_ready, 2 * g + half + 1)
                if half == 0:
                    wait(dve, ot_ready, g)
                dve.tensor_tensor(On[:, p, 2 * P * half:2 * P * (half + 1)].rearrange("p (n d) -> p n d", d=HD),
                                  O[:, :, 0:HD], rden[:, :].unsqueeze(2).broadcast_to([P, 2 * H, HD]),
                                  ALU.mult).then_inc(o_used, 1)

            def softmax1(g, p):
                dve.wait_ge(s1_ready, g + 1)
                dve.tensor_tensor(by_tile(Ss[:, p, :]), by_tile(bank[7][:, :]),
                                  mask[:, :].unsqueeze(1).broadcast_to([P, TG, P]), ALU.add).then_inc(s1_masked, 1)
                dve.wait_ge(s1_masked, g + 1)
                dve.tensor_reduce(max1[:, :], by_tile(Ss[:, p, :]), AX_X, ALU.max).then_inc(max1_ready, 1)
                dve.wait_ge(max1_ready, g + 1)
                dve.tensor_scalar(nmax1[:, p, :], max1[:, :], -SCALE1, None, ALU.mult).then_inc(sm1_ready, 1)

            def first_stats(gg):
                dve.wait_ge(x_in[gg], 16)
                row_stats(gg)
                dve.wait_ge(stats_done, gg + 1)
                aggregate(gg, gg % 2)

            first_stats(0)
            dve.wait_ge(exp_c, 1)
            link(dve.tensor_scalar(s_tok[:, :], e_tok[:, :], 1.0, None, ALU.add))
            link(dve.reciprocal(e_tok[:, :], s_tok[:, :]))
            dve.tensor_tensor(s_tok[:, :], c_tok[:, :], e_tok[:, :], ALU.mult).then_inc(silu_ready, 1)
            first_stats(1)
            dve.wait_ge(condT_ready, 1)
            dve.tensor_copy(cT[:, :], bank[1][:, 0:NB])
            dve.tensor_copy(sT[:, :], bank[1][:, NB:2 * NB]).then_inc(y_used, 1)
            dve.wait_ge(col_in, 32)
            for n, (name, i) in enumerate((("bt", 1), ("bt", 4), ("f1b", 0), ("f2b", 0))):
                dve.tensor_scalar(one_plus[:, n:n + 1], c(name, i), 1.0, None, ALU.add)
            dve.tensor_scalar(q_bias[:, :], c("bq"), SCALE0, None, ALU.mult)
            dve.tensor_copy(bcol[:, 0, :], c("bv").broadcast_to([D, D]))
            link(dve.tensor_copy(bcol[:, 1, :], c("v1b").broadcast_to([D, D])))
            dve.wait_ge(consts_ready, 1)
            link(dve.tensor_reduce(r_sums[:, :], ident[:, :].rearrange("p (n d) -> p n d", d=HD), AX_X, ALU.add))
            link(dve.tensor_reduce(r_mask[:, :], r_sums[:, :].rearrange("p (a r) -> p r a", a=HQ), AX_X, ALU.add))
            link(dve.tensor_scalar(k_bias[:, :], r_mask[:, :], c("bk"), None, ALU.mult))
            first_stats(2)
            dve.wait_ge(film_ready, 1)
            for phase, (g_, be, sh) in enumerate((("g1", "be1", 0), ("g2", "be2", 3))):
                at = slice(phase * NB, (phase + 1) * NB)
                scale_ps = bank[2][:, (2 * phase + 1) * NB:(2 * phase + 2) * NB]
                shift_ps = bank[2][:, 2 * phase * NB:(2 * phase + 1) * NB]
                dve.tensor_scalar(A[:, at], scale_ps, one_plus[:, phase:phase + 1], c(g_), ALU.add, ALU.mult)
                link(dve.tensor_scalar(t_mul[:, :], scale_ps, one_plus[:, phase:phase + 1], c(be), ALU.add, ALU.mult))
                link(dve.scalar_tensor_tensor(out=B[:, at], in0=shift_ps, scalar=c("bt", sh), in1=t_mul[:, :],
                                              op0=ALU.add, op1=ALU.add))
            for phase, (n_, f) in ((2, ("n1", "f1b")), (3, ("n2", "f2b"))):
                at = slice(phase * NB, (phase + 1) * NB)
                scale_ps = bank[3][:, (2 * phase - 4) * NB:(2 * phase - 3) * NB]
                shift_ps = bank[3][:, (2 * phase - 3) * NB:(2 * phase - 2) * NB]
                dve.tensor_scalar(A[:, at], scale_ps, one_plus[:, phase:phase + 1], c(n_), ALU.add, ALU.mult)
                last = dve.tensor_scalar(B[:, at], shift_ps, c(f, 1), None, ALU.add)
            link(last)
            dve.sem_inc(ab_ready, 1)
            modulate(0, 0)
            dve.tensor_tensor(gate_b[:, 0:D], bank[4][:, 0:D], r("gate0"), ALU.add)
            dve.tensor_tensor(gate_b[:, D:2 * D], bank[4][:, D:2 * D], r("gate1"), ALU.add).then_inc(gate_ready, 1)
            modulate(1, 1)
            dve.wait_ge(fold_ready, 1)
            dve.tensor_copy(vT[:, :], bank[5][:, 0:D]).then_inc(fold_copied, 1)
            dve.wait_ge(fold_ready, 2)
            dve.tensor_copy(wvp[:, :], bank[5][:, D:2 * D])
            dve.tensor_tensor(r("bproj0"), bank[5][:, 2 * D:3 * D], r("bproj0"), ALU.add)
            dve.tensor_tensor(r("bproj1"), bank[5][:, 3 * D:4 * D], r("bproj1"), ALU.add).then_inc(rows_ready, 1)
            dve.wait_ge(x_in[3], 16)
            dve.wait_ge(x_in[4], 16)

            def attention0(g, p):
                scores_max(g, 0)
                if not (isinstance(g, int) and g == 0):
                    normalise(g - 1, 1 - p, 1)
                scores_max(g, 1)
                row_stats(g + 3)
                modulate(g + 2, p, g + 3)
                aggregate(g + 3, 1 - p)
                scores_max(g, 2)
                normalise(g, p, 0)
                scores_max(g, 3)
                if not (isinstance(g, int) and g == 0):
                    update(0, g - 1, 1 - p)
                if isinstance(g, int) and g == 0:
                    dve.wait_ge(gates_in, 16 * TB)

            def mlp(phase):
                def step(g, p):
                    gg = phase * NG + g
                    if isinstance(g, int) and g == 0:
                        if phase == 1:
                            normalise(7, 1, 1)
                        else:
                            softmax1(7, 1)
                    if phase < 3 or not isinstance(g, int) or g < 5:
                        row_stats(gg + 3)
                        modulate(gg + 2, p, gg + 3)
                        aggregate(gg + 3, 1 - p)
                    elif g < 6:
                        modulate(gg + 2, p)
                    if isinstance(g, int) and g == 0:
                        update(phase - 1, 7, 1)
                    else:
                        update(phase, g - 1, 1 - p)
                return step

            def attention1(g, p):
                if not (isinstance(g, int) and g == 0):
                    softmax1(g - 1, 1 - p)
                row_stats(2 * NG + g + 3)
                modulate(2 * NG + g + 2, p, 2 * NG + g + 3)
                aggregate(2 * NG + g + 3, 1 - p)
                if isinstance(g, int) and g == 0:
                    update(1, 7, 1)
                else:
                    update(2, g - 1, 1 - p)

            group_steps(dve, attention0)
            group_steps(dve, mlp(1))
            group_steps(dve, attention1)
            group_steps(dve, mlp(3), 4)
            update(3, 7, 1)

        @block.scalar
        def _(act):
            act.dma_start(col[:, :], columns).then_inc(col_in, 16)
            act.dma_start(row[:, :, :], rows.unsqueeze(0).broadcast_to([P, len(R_NAMES), D])).then_inc(col_in, 16)
            cut = [0, W_AT["Wproj"][0], W_AT["W1_0"][0], W_ALL]
            for s_in, lo, hi in zip((wt_in, wrest_in, wmlp_in), cut, cut[1:]):
                act.dma_start(W[:, lo:hi], weights[:, lo:hi]).then_inc(s_in, 16)
            act.wait_ge(cond_in, 16)
            act.activation(e_tok[:, :], c_tok[:, :], ACT.Exp, scale=-1.0).then_inc(exp_c, 1)

            def apply(gg, p):
                act.wait_ge(rstd_ready, gg + 1)
                wait(act, hT_ready, gg - 1)
                for t in range(TG):
                    last = act.activation(xhat[:, p, P * t:P * (t + 1)], X[:, x_tile(gg, t), :], ACT.Identity,
                                          bias=shift[:, p, t:t + 1], scale=rstd[:, p, t:t + 1])
                last.then_inc(xhat_ready, 1)

            def move_q(g, p, k):
                act.wait_ge(qkv_ready, 3 * g + 1)
                wait(act, q_spread[p], 16 * HQ * k)
                act.activation(Qs[:, p, :], bank[2][:, :], ACT.Identity, bias=q_bias[:, :], scale=SCALE0).then_inc(qkv_moved, 1)

            def move_k(g, p):
                act.wait_ge(qkv_ready, 3 * g + 2)
                wait(act, s_ready, 4 * g - 4)
                for q in range(HQ):
                    last = act.activation(Kx[:, p, q, :], bank[3][:, :], ACT.Identity, bias=k_bias[:, q:q + 1],
                                          scale=r_mask[:, q:q + 1])
                    last.then_inc(kx_ready, 1)

            def move_v(g, p, k):
                act.wait_ge(qkv_ready, 3 * g + 3)
                wait(act, v_stored[p], 16 * k)
                vs = Vs[:, p, :].rearrange("p (n w) -> p n w", w=VW)
                act.activation(vs[:, :, 0:HD], bank[2][:, :].rearrange("p (n d) -> p n d", d=HD),
                               ACT.Copy).then_inc(qkv_moved, 1)

            def exps(g, t):
                tile = 4 * g + t
                act.wait_ge(st_ready, tile + 1)
                wait(act, pv_done, tile - 3)
                act.activation(PT[:, t, :], St[:, t % 2, :], ACT.Exp).then_inc(pt_ready, 1)

            def move_o(g, p):
                act.wait_ge(ot_ready, g + 1)
                act.activation(OTs[:, p, :], bank[1][:, :], ACT.Copy).then_inc(ot_moved, 1)

            def gelus(m, p):
                for n in range(NC):
                    act.wait_ge(u_ready, NC * m + n + 1)
                    bias = c("b1_0" if m_layer[0] == 0 else "b1_1", n)
                    act.activation(gT[:, p, n, :], bank[2 + n][:, :], ACT.Gelu, bias=bias).then_inc(g_ready, 1)

            m_layer = [0]
            apply(0, 0)
            apply(1, 1)
            apply(2, 0)
            act.wait_ge(ab_ready, 1)
            move_q(0, 0, 0)
            move_k(0, 0)
            move_v(0, 0, 0)

            def attention0(g, p, k=0):
                more = not (isinstance(g, int) and g == NG - 1)
                if more:
                    move_q(g + 1, 1 - p, k)
                exps(g, 0)
                if more:
                    move_k(g + 1, 1 - p)
                exps(g, 1)
                if more:
                    move_v(g + 1, 1 - p, k)
                if not (isinstance(g, int) and g == 0):
                    move_o(g - 1, 1 - p)
                exps(g, 2)
                exps(g, 3)
                apply(g + 3, 1 - p)

            attention0(0, 0, 0)
            with act.Fori(0, 3) as i:
                attention0(i * 2 + 1, 1, i + 1)
                attention0(i * 2 + 2, 0, i + 1)
            attention0(7, 1)

            def mlp(phase):
                def step(g, p):
                    m_layer[0] = phase // 2
                    m = (phase // 2) * NG + g
                    if isinstance(g, int) and g == 0 and phase == 3:
                        exps1(7, 1)
                    gelus(m, p)
                    if isinstance(g, int) and g == 0:
                        if phase == 1:
                            move_o(7, 1)
                        else:
                            move_p1(7, 1)
                    if phase < 3 or not isinstance(g, int) or g < 5:
                        apply(phase * NG + g + 3, 1 - p)
                return step

            def exps1(g, p):
                act.wait_ge(sm1_ready, g + 1)
                act.wait_ge(x_updated, 2 * NG + g)
                for t in range(TG):
                    last = act.activation(St[:, p, P * t:P * (t + 1)], Ss[:, p, P * t:P * (t + 1)], ACT.Exp,
                                          scale=SCALE1, bias=nmax1[:, p, t:t + 1], accum_out=den1[:, p, t:t + 1])
                last.then_inc(p1_ready, 1)

            def move_p1(g, p):
                act.wait_ge(p1T_ready, g + 1)
                act.activation(PT[:, p, :], bank[6][:, :], ACT.Copy).then_inc(p1T_moved, 1)

            def move_qkv1(g, p, which):
                act.wait_ge(qkv1_ready, 3 * g + which + 1)
                if which == 0:
                    act.activation(Qs[:, p, :], bank[2][:, :], ACT.Identity, bias=c("q1b")).then_inc(qkv1_moved, 1)
                elif which == 1:
                    act.activation(Kx[:, p, 0, :], bank[3][:, :], ACT.Identity, bias=c("k1b")).then_inc(qkv1_moved, 1)
                else:
                    act.activation(Vs[:, p, 0:GN], bank[4][:, :], ACT.Copy).then_inc(qkv1_moved, 1)

            def attention1(g, p):
                first = isinstance(g, int) and g == 0
                if not first:
                    exps1(g - 1, 1 - p)
                move_qkv1(g, p, 0)
                if not first:
                    move_p1(g - 1, 1 - p)
                move_qkv1(g, p, 1)
                move_qkv1(g, p, 2)
                apply(2 * NG + g + 3, 1 - p)

            group_steps(act, mlp(1))
            group_steps(act, attention1)
            group_steps(act, mlp(3), 4)

        @block.tensor
        def _(pe):
            pe.wait_ge(consts_ready, 1)
            pe.wait_ge(silu_ready, 1)
            pe.transpose(bank[1][:, 0:NB], c_tok[:, :], ident[:, :])
            pe.transpose(bank[1][:, NB:2 * NB], s_tok[:, :], ident[:, :]).then_inc(condT_ready, 1)

            def rows_T(gg, p):
                pe.wait_ge(xhat_ready, gg + 1)
                wait(pe, hA_ready, gg)
                for t in range(TG):
                    last = pe.transpose(hT_ps[:, P * t:P * (t + 1)], xhat[:, p, P * t:P * (t + 1)], ident[:, :])
                last.then_inc(hT_ready, 1)

            rows_T(0, 0)
            pe.wait_ge(y_used, 1)
            pe.wait_ge(wt_in, 16)
            for n, i in enumerate((0, 1, 3, 4)):
                pe.matmul(bank[2][:, n * NB:(n + 1) * NB], w("Wt", i), sT[:, :], start=True, stop=True)
            for n, name in enumerate(("film1", "film2")):
                for i in range(2):
                    pe.matmul(bank[3][:, (2 * n + i) * NB:(2 * n + i + 1) * NB], w(name, i), cT[:, :], start=True, stop=True)
            for n, i in enumerate((2, 5)):
                last = pe.matmul(bank[4][:, n * D:(n + 1) * D], sT[:, :], w("Wt", i), start=True, stop=True)
            last.then_inc(film_ready, 1)
            pe.wait_ge(wrest_in, 16)
            rows_T(1, 1)
            pe.transpose(bank[5][:, 0:D], w("v1"), ident[:, :]).then_inc(fold_ready, 1)

            def queries0(g, p):
                pe.wait_ge(h_ready, g + 1)
                wait(pe, qkv_moved, 2 * g)
                pe.matmul(bank[2][:, :], w("Wqkv", 0), h[:, p, :], start=True, stop=True).then_inc(qkv_ready, 1)

            def keys0(g, p):
                wait(pe, kx_ready, HQ * g)
                pe.matmul(bank[3][:, :], w("Wqkv", 1), h[:, p, :], start=True, stop=True).then_inc(qkv_ready, 1)

            def values0(g, p):
                pe.wait_ge(qkv_moved, 2 * g + 1)
                for t in range(TG):
                    last = pe.matmul(bank[2][:, P * t:P * (t + 1)], h[:, p, P * t:P * (t + 1)], w("Wqkv", 2),
                                     start=True, stop=True)
                last.then_inc(qkv_ready, 1)

            def scores0(g, p, t):
                tile = 4 * g + t
                wait(pe, s_used, tile - 1)
                for b in range(TB):
                    at = P * t + L * b
                    last = pe.matmul(bank[4 + t % 2][:, P * b:P * (b + 1)], Qx[:, p, TB * t + b, :, :].rearrange("p a t -> p (a t)"), Kx[:, p, :, at:at + L],
                                     start=True, stop=True)
                last.then_inc(s_ready, 1)

            def weigh0(g, p, t):
                tile = 4 * g + t
                pe.wait_ge(pt_ready, tile + 1)
                if t % 2 == 0:
                    wait(pe, o_used, 2 * g - 1 + t // 2)
                for q in range(HQ):
                    for b in range(TB):
                        at = (t % 2) * OW + q * HQ * VW
                        last = pe.matmul(bank[6 + t // 2][L * b:L * (b + 1), at:at + HQ * VW],
                                         PT[:, t, P * b + L * q:P * b + L * (q + 1)],
                                         Vx[:, p, TB * t + b, :, VW * q:VW * (q + 1)], start=True, stop=True)
                last.then_inc(pv_done, 1)

            def output_T(g, p):
                pe.wait_ge(o_used, 2 * g + 2)
                pe.wait_ge(y_used, g + 1)
                for t in range(TG):
                    last = pe.transpose(bank[1][:, P * t:P * (t + 1)], On[:, p, P * t:P * (t + 1)], ident[:, :])
                last.then_inc(ot_ready, 1)

            def project0(g, p):
                pe.wait_ge(ot_moved, g + 1)
                for t in range(TG):
                    last = pe.matmul(y_ps[:, P * t:P * (t + 1)], OTs[:, p, P * t:P * (t + 1)], w("Wproj"),
                                     start=True, stop=True)
                last.then_inc(y_ready, 1)

            queries0(0, 0)
            keys0(0, 0)
            values0(0, 0)
            pe.wait_ge(fold_copied, 1)
            pe.matmul(bank[5][:, D:2 * D], vT[:, :], w("proj1"), start=True, stop=True)
            pe.matmul(bank[5][:, 2 * D:3 * D], bcol[:, 0, :], w("Wproj"), start=True, stop=True)
            pe.matmul(bank[5][:, 3 * D:4 * D], bcol[:, 1, :], w("proj1"), start=True, stop=True).then_inc(fold_ready, 1)
            pe.wait_ge(q_spread[0], 16 * HQ)
            pe.wait_ge(kx_ready, HQ)
            scores0(0, 0, 0)
            pe.wait_ge(rows_ready, 1)
            scores0(0, 0, 1)

            def attention0(g, p, k=None):
                first = isinstance(g, int) and g == 0
                more = not (isinstance(g, int) and g == NG - 1)
                if more:
                    queries0(g + 1, 1 - p)
                scores0(g, p, 2)
                if more:
                    keys0(g + 1, 1 - p)
                pe.wait_ge(v_spread[p], 16 * HQ * (k if p else k + 1))
                weigh0(g, p, 0)
                scores0(g, p, 3)
                if more:
                    values0(g + 1, 1 - p)
                if not first:
                    output_T(g - 1, 1 - p)
                rows_T(g + 2, p)
                weigh0(g, p, 1)
                if more:
                    pe.wait_ge(q_spread[1 - p], 16 * HQ * (k + 1))
                    pe.wait_ge(kx_ready, HQ * (g + 2))
                    scores0(g + 1, 1 - p, 0)
                if not first:
                    project0(g - 1, 1 - p)
                weigh0(g, p, 2)
                if more:
                    scores0(g + 1, 1 - p, 1)
                weigh0(g, p, 3)

            attention0(0, 0, 0)
            with pe.Fori(0, 3) as i:
                attention0(i * 2 + 1, 1, i + 1)
                attention0(i * 2 + 2, 0, i + 1)
            attention0(7, 1, 4)

            def up(phase, g, p):
                m = (phase // 2) * NG + g
                pe.wait_ge(h_ready, phase * NG + g + 1)
                for n in range(NC):
                    wait(pe, g_ready, NC * (m - 1) + n + 1)
                    last = pe.matmul(bank[2 + n][:, :], w(f"W1_{phase // 2}", n), h[:, p, :], start=True, stop=True)
                    last.then_inc(u_ready, 1)

            def down(phase, g, p):
                gg, m = phase * NG + g, (phase // 2) * NG + g
                pe.wait_ge(g_ready, NC * (m + 1))
                if phase == 1:
                    pe.wait_ge(y_used, gg + 1)
                else:
                    pe.wait_ge(x_updated, gg + 1)
                for t in range(TG):
                    for n in range(NC):
                        last = pe.matmul(y_ps[:, P * t:P * (t + 1)], gT[:, p, n, P * t:P * (t + 1)],
                                         w(f"W2_{phase // 2}", n), start=(n == 0), stop=(n == NC - 1))
                last.then_inc(y_ready, 1)

            def qkv1(g, p):
                pe.wait_ge(h_ready, 2 * NG + g + 1)
                wait(pe, qkv1_moved, 3 * g)
                pe.matmul(bank[2][:, :], w("q1"), h[:, p, :], start=True, stop=True).then_inc(qkv1_ready, 1)
                pe.matmul(bank[3][:, :], w("k1"), h[:, p, :], start=True, stop=True).then_inc(qkv1_ready, 1)
                for t in range(TG):
                    last = pe.matmul(bank[4][:, P * t:P * (t + 1)], h[:, p, P * t:P * (t + 1)], wvp[:, :],
                                     start=True, stop=True)
                last.then_inc(qkv1_ready, 1)

            def scores1(g, p):
                pe.wait_ge(qkv1_moved, 3 * g + 3)
                for t in range(TG):
                    at = slice(P * t, P * (t + 1))
                    last = pe.matmul(bank[7][:, at], Qs[:, p, at], Kx[:, p, 0, at], start=True, stop=True)
                last.then_inc(s1_ready, 1)

            def probs_T(g, p):
                pe.wait_ge(p1_ready, g + 1)
                for t in range(TG):
                    last = pe.transpose(bank[6][:, P * t:P * (t + 1)], St[:, p, P * t:P * (t + 1)], ident[:, :])
                last.then_inc(p1T_ready, 1)

            def values1(g, p):
                pe.wait_ge(p1T_moved, g + 1)
                pe.wait_ge(x_updated, 2 * NG + g + 1)
                for t in range(TG):
                    at = slice(P * t, P * (t + 1))
                    last = pe.matmul(y_ps[:, at], PT[:, p, at], Vs[:, p, at], start=True, stop=True)
                last.then_inc(y_ready, 1)

            def mlp(phase):
                def step(g, p):
                    gg = phase * NG + g
                    first = isinstance(g, int) and g == 0
                    if first and phase == 3:
                        scores1(7, 1)
                    up(phase, g, p)
                    if first and phase == 1:
                        output_T(7, 1)
                    if first and phase == 3:
                        probs_T(7, 1)
                    if phase < 3 or not isinstance(g, int) or g < 6:
                        rows_T(gg + 2, p)
                    if not first:
                        down(phase, g - 1, 1 - p)
                    elif phase == 1:
                        project0(7, 1)
                    else:
                        values1(7, 1)
                return step

            def attention1(g, p):
                first = isinstance(g, int) and g == 0
                if first:
                    rows_T(2 * NG + g + 2, p)
                    down(1, 7, 1)
                    qkv1(0, 0)
                else:
                    scores1(g - 1, 1 - p)
                    qkv1(g, p)
                    probs_T(g - 1, 1 - p)
                    rows_T(2 * NG + g + 2, p)
                    values1(g - 1, 1 - p)

            pe.wait_ge(s_used, 4 * NG)
            pe.wait_ge(wmlp_in, 16)
            group_steps(pe, mlp(1))
            group_steps(pe, attention1)
            group_steps(pe, mlp(3), 4)
            down(3, 7, 1)


def kernel(x, cond_1024, L0_cond_Wqkv, L0_cond_bqkv, L0_cond_Wproj, L0_cond_bproj, L0_cond_W1, L0_cond_b1,
           L0_cond_W2, L0_cond_b2, L0_cond_Wt, L0_cond_bt, L0_cond_g1, L0_cond_be1, L0_cond_g2, L0_cond_be2,
           L1_cond_norm1_w, L1_cond_film1_w, L1_cond_film1_b, L1_cond_q_w, L1_cond_q_b, L1_cond_k_w, L1_cond_k_b,
           L1_cond_v_w, L1_cond_v_b, L1_cond_proj_w, L1_cond_proj_b, L1_cond_norm2_w, L1_cond_film2_w,
           L1_cond_film2_b, L1_cond_mlp_w1, L1_cond_mlp_b1, L1_cond_mlp_w2, L1_cond_mlp_b2):
    import numpy as np
    import concourse.bacc as bacc
    from concourse.bass_utils import run_bass_kernel_spmd

    def by_a(m):
        return m.reshape(m.shape[:-1] + (HQ, HQ, HD)).swapaxes(-3, -2).reshape(m.shape)

    def chunks(m):
        return m.reshape(-1, P, m.shape[-1]).swapaxes(0, 1).reshape(P, -1)

    wqkv = np.asarray(L0_cond_Wqkv).reshape(D, 3, D)
    bqkv = np.asarray(L0_cond_bqkv).reshape(3, D)
    bt = np.asarray(L0_cond_bt).reshape(6, D)
    ws = {"Wt": L0_cond_Wt, "film1": L1_cond_film1_w, "film2": L1_cond_film2_w, "Wproj": L0_cond_Wproj,
          "v1": L1_cond_v_w, "proj1": L1_cond_proj_w, "Wqkv": by_a(wqkv).reshape(D, 3 * D), "W1_0": L0_cond_W1,
          "W2_0": chunks(np.asarray(L0_cond_W2)), "q1": L1_cond_q_w, "k1": L1_cond_k_w, "W1_1": L1_cond_mlp_w1,
          "W2_1": chunks(np.asarray(L1_cond_mlp_w2))}
    cs = {"bt": bt, "g1": L0_cond_g1, "be1": L0_cond_be1, "g2": L0_cond_g2, "be2": L0_cond_be2, "bq": by_a(bqkv[0]),
          "bk": by_a(bqkv[1]), "bv": bqkv[2], "b1_0": L0_cond_b1, "n1": L1_cond_norm1_w, "n2": L1_cond_norm2_w,
          "f1b": L1_cond_film1_b, "f2b": L1_cond_film2_b, "q1b": L1_cond_q_b, "k1b": L1_cond_k_b, "v1b": L1_cond_v_b,
          "b1_1": L1_cond_mlp_b1}
    rs = {"gate0": bt[2], "gate1": bt[5], "bproj0": L0_cond_bproj, "b2_0": L0_cond_b2, "bproj1": L1_cond_proj_b,
          "b2_1": L1_cond_mlp_b2}
    arrays = {
        "x": np.ascontiguousarray(np.asarray(x).reshape(NB * L, D)),
        "cond": np.ascontiguousarray(np.asarray(cond_1024)),
        "weights": np.ascontiguousarray(np.concatenate([np.asarray(ws[n]) for n, _ in W_NAMES], axis=1)),
        "columns": np.ascontiguousarray(np.concatenate([np.asarray(cs[n]).reshape(-1, D) for n, _ in C_NAMES], axis=0).T),
        "rows": np.ascontiguousarray(np.stack([np.asarray(rs[n]) for n in R_NAMES])),
    }
    nc = bacc.Bacc("TRN2", target_bir_lowering=False, num_devices=1)
    aps = [nc.dram_tensor(n, a.shape, mybir.dt.from_np(a.dtype), kind="ExternalInput").ap() for n, a in arrays.items()]
    out = nc.dram_tensor("out", (NB * L, D), F32, kind="ExternalOutput").ap()
    build(nc, *aps, out)
    result = run_bass_kernel_spmd(nc, [arrays], core_ids=[0])
    return result.results[0]["out"].reshape(NB, L, D)
```

```python
from contextlib import ExitStack

import concourse.bass as bass
from concourse import mybir

F32 = mybir.dt.float32
ALU = mybir.AluOpType
ACT = mybir.ActivationFunctionType
AX_X = mybir.AxisListType.X

P = 128
D = 128
NB = 128
L = 32
H, HD = 16, 8
FF = 512
NC = FF // P
TB = P // L
NT = NB * L // P
TG = 4
NG = NT // TG
GB = TG * TB
GN = TG * P
HQ = 4
VW = HD + 1
OW = H * VW
SCALE0 = HD ** -0.5
SCALE1 = D ** -0.5
OFF_BLOCK = -1.0e30

W_NAMES = [("Wt", 6 * D), ("film1", 2 * D), ("film2", 2 * D), ("Wproj", D), ("v1", D), ("proj1", D),
           ("Wqkv", 3 * D), ("W1_0", FF), ("W2_0", FF), ("q1", D), ("k1", D), ("W1_1", FF), ("W2_1", FF)]
W_AT, W_ALL = {}, 0
for _name, _n in W_NAMES:
    W_AT[_name] = (W_ALL, _n)
    W_ALL += _n
C_NAMES = [("bt", 6), ("g1", 1), ("be1", 1), ("g2", 1), ("be2", 1), ("bq", 1), ("bk", 1), ("bv", 1), ("b1_0", NC),
           ("n1", 1), ("n2", 1), ("f1b", 2), ("f2b", 2), ("q1b", 1), ("k1b", 1), ("v1b", 1), ("b1_1", NC)]
C_AT, C_ALL = {}, 0
for _name, _n in C_NAMES:
    C_AT[_name] = (C_ALL, _n)
    C_ALL += _n
R_NAMES = ["gate0", "gate1", "bproj0", "b2_0", "bproj1", "b2_1"]


def build(nc, x, cond, weights, columns, rows, out):
    with ExitStack() as ctx:
        def sb(name, shape):
            return ctx.enter_context(nc.sbuf_tensor(name, shape, F32))

        def sem(name):
            return ctx.enter_context(nc.semaphore(name))

        gates_d = nc.dram_tensor("gates_scratch", [NB, 2 * D], F32, kind="Internal").ap()
        values_d = nc.dram_tensor("values_scratch", [2, GN, OW], F32, kind="Internal").ap()

        X = sb("X", [P, NT, D])
        gate = sb("gate", [P, NT, 2 * D])
        W = sb("W", [P, W_ALL])
        col = sb("col", [P, C_ALL])
        row = sb("row", [P, len(R_NAMES), D])
        c_tok, eT, warm = sb("c_tok", [NB, D]), sb("eT", [D, NB]), sb("warm", [P, 1])
        cT, sT = sb("cT", [D, NB]), sb("sT", [D, NB])
        A, B = sb("A", [D, 4 * NB]), sb("B", [D, 4 * NB])
        t_mul, one_plus = sb("t_mul", [D, NB]), sb("one_plus", [D, 8])
        gate_b = sb("gate_b", [NB, 2 * D])
        vT, wvp, bcol = sb("vT", [D, D]), sb("wvp", [D, D]), sb("bcol", [D, 2, D])
        q_bias, k_bias, r_sums, r_mask = sb("q_bias", [D, 1]), sb("k_bias", [D, HQ]), sb("r_sums", [D, H]), sb("r_mask", [D, HQ])
        ident, mask, minus_half = (
            sb("ident", [P, P]), sb("mask", [P, P]), sb("minus_half", [P, TG]))
        kind = sb("kind", [P, 3, 4 * NG])
        stats, mv = sb("stats", [P, TG, 6]), sb("mv", [P, TG, 2])
        v_sb, mk, rstd, shift = (sb(n, [P, 2, TG]) for n in ("v_sb", "mk", "rstd", "shift"))
        sqm = sb("sqm", [P, TG])
        xhat = sb("xhat", [P, 2, GN])
        hA, h = sb("hA", [P, 2, GN]), sb("h", [P, 2, GN])
        Qs = sb("Qs", [P, 2, GN])
        Vs = sb("Vs", [P, 2, TG * OW])
        Qx = sb("Qx", [P, 2, GB, HQ, L])
        Kx = sb("Kx", [P, 2, HQ, GN])
        Vx = sb("Vx", [P, 2, GB, HQ, HQ * VW])
        smax = sb("smax", [P, 2, TB * HQ])
        Sc = sb("Sc", [P, GN])
        Ss, St = sb("Ss", [P, 2, GN]), sb("St", [P, 2, GN])
        PT = sb("PT", [P, TG, GN])
        rden, On, OTs = sb("rden", [P, 2, 2 * H]), sb("On", [P, 2, GN]), sb("OTs", [P, 2, GN])
        xg, yG, gb = sb("xg", [P, 2, GN]), sb("yG", [P, GN]), sb("gb", [P, GN])
        max1, nmax1 = sb("max1", [P, TG]), sb("nmax1", [P, 2, TG])
        den1, rden1 = sb("den1", [P, 2, TG]), sb("rden1", [P, TG])
        gT = Qx[:, :, :, :, :].rearrange("p v (n b) a t -> p v n (b a t)", n=NC)

        bank = [ctx.enter_context(nc.psum_tensor(f"bank{i}", [P, 512], F32)) for i in range(8)]
        hT_ps, y_ps = bank[0], bank[1]

        x_in = [sem(f"x_in{i}") for i in range(5)]
        cond_in, col_in, row_in, wt_in, wrest_in, wmlp_in = (sem(n) for n in ("cond_in", "col_in", "row_in", "wt_in", "wrest_in", "wmlp_in"))
        consts_ready, zeros_ready = sem("consts_ready"), sem("zeros_ready")
        exp_c, dve_pre, bias_ready = sem("exp_c"), sem("dve_pre"), sem("bias_ready")
        condT_ready, ct_ready = sem("condT_ready"), sem("ct_ready")
        film_ready, gate_ready, ab_ready = sem("film_ready"), sem("gate_ready"), sem("ab_ready")
        gates_stored = sem("gates_stored")
        gates_in = [sem(f"gates_in{i}") for i in range(3)]
        fold_ready, fold_copied, rows_ready = sem("fold_ready"), sem("fold_copied"), sem("rows_ready")
        stats_done, mv_done, v_ready, rstd_ready = sem("stats_done"), sem("mv_done"), sem("v_ready"), sem("rstd_ready")
        pool_chain, dve_chain = sem("pool_chain"), sem("dve_chain")
        xhat_ready, hT_ready, hA_ready, h_ready = (
            sem(n) for n in ("xhat_ready", "hT_ready", "hA_ready", "h_ready"))
        gb_ready, xg_ready, y_ready, y_used, x_updated = (
            sem(n) for n in ("gb_ready", "xg_ready", "y_ready", "y_used", "x_updated"))
        qkv_ready, qkv_moved, kx_ready = sem("qkv_ready"), sem("qkv_moved"), sem("kx_ready")
        q0_placed = sem("q0_placed")
        q_spread = [sem(f"q_spread{i}") for i in range(2)]
        v_stored = [sem(f"v_stored{i}") for i in range(2)]
        v_spread = [sem(f"v_spread{i}") for i in range(2)]
        s_copied = sem("s_copied")
        s_ready, smax_ready, st_ready, pt_ready, pv_done = (
            sem(n) for n in ("s_ready", "smax_ready", "st_ready", "pt_ready", "pv_done"))
        s_used = [sem(f"s_used{i}") for i in range(2)]
        rden_ready, o_used, ot_ready, ot_moved = (sem(n) for n in ("rden_ready", "o_used", "ot_ready", "ot_moved"))
        qkv1_ready, qkv1_moved, s1_ready, s1_masked, max1_ready, sm1_ready, p1_ready, p1T_ready, p1T_moved, rden1_ready = (
            sem(n) for n in ("qkv1_ready", "qkv1_moved", "s1_ready", "s1_masked", "max1_ready", "sm1_ready", "p1_ready", "p1T_ready",
                             "p1T_moved", "rden1_ready"))
        u_ready, g_ready = sem("u_ready"), sem("g_ready")
        out_done = sem("out_done")


        def w(name, i=0, n=D):
            at = W_AT[name][0] + i * n
            return W[:, at:at + n]

        def c(name, i=0):
            at = C_AT[name][0] + i
            return col[:, at:at + 1]

        def r(name):
            return row[:, R_NAMES.index(name), :]

        def by_tile(ap):
            return ap.rearrange("p (t d) -> p t d", t=TG)

        def by_seq(ap):
            return ap.rearrange("p (b t) -> p b t", t=L)

        def wait(eng, s, n):
            if not isinstance(n, int) or n > 0:
                eng.wait_ge(s, n)

        def group_steps(eng, step, first=1, turns=3):
            for g in range(first):
                step(g, g % 2)
            with eng.Fori(0, turns) as i:
                step(i * 2 + first, first % 2)
                step(i * 2 + first + 1, (first + 1) % 2)
            for g in range(first + 2 * turns, NG):
                step(g, g % 2)

        def known(g, low, high):
            return not isinstance(g, int) or low <= g < high

        def x_group(gg):
            if isinstance(gg, int):
                g = gg % NG
                return slice(g * TG, (g + 1) * TG)
            return bass.ds(((gg) % NG) * TG, TG)

        def x_tile(gg, t):
            if isinstance(gg, int):
                return slice((gg % NG) * TG + t, (gg % NG) * TG + t + 1)
            return bass.ds((gg % NG) * TG + t, 1)

        def seqs(gg):
            if isinstance(gg, int):
                return slice(gg * GB, (gg + 1) * GB)
            return bass.ds(gg * GB, GB)

        def one(gg):
            return slice(gg, gg + 1) if isinstance(gg, int) else bass.ds(gg, 1)

        block = ctx.enter_context(nc.Block())

        @block.sync
        def _(sp):
            xv = x.rearrange("(i p) d -> p i d", p=P)
            ov = out.rearrange("(i p) d -> p i d", p=P)
            sp.dma_start(c_tok[:, :], cond).then_inc(cond_in, 16)
            sp.dma_start(X[:, 0:TG, :], xv[:, 0:TG, :]).then_inc(x_in[0], 16)
            lo, hi = W_AT["Wt"][0], W_AT["Wproj"][0]
            sp.dma_start(W[:, lo:hi], weights[:, lo:hi]).then_inc(wt_in, 16)
            for g in range(1, 4):
                sp.dma_start(X[:, TG * g:TG * (g + 1), :], xv[:, TG * g:TG * (g + 1), :]).then_inc(x_in[g], 16)
            sp.dma_start(X[:, 4 * TG:, :], xv[:, 4 * TG:, :]).then_inc(x_in[4], 16)

            def spread_q(g, p):
                wait(sp, s_ready, 4 * g - 4)
                sp.wait_ge(qkv_moved, 2 * g + 1)
                for a in range(HQ):
                    sp.dma_start(Qx[L * a:L * (a + 1), p, :, a, :], by_seq(Qs[L * a:L * (a + 1), p, :])).then_inc(q_spread[p], 16)

            def spread_v(g, p, k):
                sp.wait_ge(qkv_moved, 2 * g + 2)
                wait(sp, pv_done, 4 * g - 4)
                sp.dma_start(values_d[p].rearrange("(t x) w -> x t w", x=P),
                             Vs[:, p, :].rearrange("p (t w) -> p t w", t=TG)).then_inc(v_stored[p], 16)
                sp.wait_ge(v_stored[p], 16 * (k + 1))
                src = values_d[p].rearrange("(b l) (a w) -> a l b w", l=L, a=HQ)
                for a in range(HQ):
                    sp.dma_start(Vx[L * a:L * (a + 1), p, :, a, :], src[a]).then_inc(v_spread[p], 16)

            sp.wait_ge(gate_ready, 1)
            sp.dma_start(gates_d, gate_b[:, :]).then_inc(gates_stored, 16)
            sp.wait_ge(zeros_ready, 2)
            spread_v(0, 0, 0)
            sp.wait_ge(zeros_ready, 3)
            spread_q(1, 1)
            sp.wait_ge(gates_stored, 16)
            src = gates_d.rearrange("(i b) d -> b i d", b=TB)

            def spread_gates(n, i, tiles):
                for b in range(TB):
                    sp.dma_start(gate[L * b:L * (b + 1), tiles, D * i:D * (i + 1)],
                                 src[b:b + 1, tiles, D * i:D * (i + 1)].broadcast_to([L, tiles.stop - tiles.start, D])).then_inc(gates_in[n], 16)

            spread_gates(0, 0, slice(0, NT // 2))
            spread_v(1, 1, 0)
            spread_q(2, 0)
            spread_gates(1, 0, slice(NT // 2, NT))
            with sp.Fori(0, 2) as i:
                spread_v(i * 2 + 2, 0, i + 1)
                spread_q(i * 2 + 3, 1)
                spread_v(i * 2 + 3, 1, i + 1)
                spread_q(i * 2 + 4, 0)
            spread_v(6, 0, 3)
            spread_q(7, 1)
            spread_v(7, 1, 3)
            spread_gates(2, 1, slice(0, NT))

            for g in range(NG - 1):
                sp.wait_ge(x_updated, 3 * NG + 2 + g)
                sp.dma_start(ov[:, x_group(g), :], X[:, x_group(g), :]).then_inc(out_done, 16)
            for half in range(2):
                sp.wait_ge(x_updated, 4 * NG + 1 + half)
                tiles = slice(NT - TG + 2 * half, NT - TG + 2 * half + 2)
                sp.dma_start(ov[:, tiles, :], X[:, tiles, :]).then_inc(out_done, 16)
            sp.wait_ge(out_done, 16 * (NG + 1))

        @block.gpsimd
        def _(pool):
            pool.memset(ident[:, :], 0.0)
            pool.memset(minus_half[:, :], -0.5).then_inc(pool_chain, 1)
            pool.wait_ge(pool_chain, 1)
            pool.affine_select(out=ident[:, :], in_=ident[:, :], compare_op=ALU.not_equal, fill=1.0, base=0,
                               pattern=[[-1, P]], channel_multiplier=1).then_inc(consts_ready, 1)

            def power(gg, p):
                pool.wait_ge(v_ready, gg + 1)
                wait(pool, xhat_ready, gg - 1)
                pool.tensor_tensor(rstd[:, p, :], v_sb[:, p, :], minus_half[:, :], ALU.pow).then_inc(pool_chain, 1)
                pool.wait_ge(pool_chain, gg + 2)
                pool.tensor_tensor(shift[:, p, :], mk[:, p, :], rstd[:, p, :], ALU.mult).then_inc(rstd_ready, 1)

            def add_shift(gg, p, phase=0, g=-1):
                pool.wait_ge(hA_ready, gg + 1)
                if phase == 0:
                    wait(pool, qkv_ready, 3 * (g + 1))
                elif phase == 2:
                    pool.wait_ge(qkv1_ready, 3 * (g + 1))
                else:
                    pool.wait_ge(u_ready, NC * ((phase // 2) * NG + g + 1))
                pool.tensor_tensor(by_seq(h[:, p, :]), by_seq(hA[:, p, :]),
                                   B[:, seqs(gg)].unsqueeze(2).broadcast_to([P, GB, L]), ALU.add).then_inc(h_ready, 1)

            def subtract_max(g, t):
                tile = 4 * g + t
                pool.wait_ge(smax_ready, tile + 1)
                pool.tensor_tensor(by_seq(Ss[:, 1, :]), by_seq(Sc[:, :]),
                                   smax[:, 1, :].unsqueeze(2).broadcast_to([P, TB * HQ, L]),
                                   ALU.subtract).then_inc(s_used[1], 1)

            def keep(phase, g, p):
                gg = phase * NG + g
                bias = r(["bproj0", "b2_0", "bproj1", "b2_1"][phase]).unsqueeze(1).broadcast_to([P, TG, D])
                wait(pool, x_updated, gg)
                if phase < 2:
                    wait(pool, xg_ready, gg)
                    pool.tensor_tensor(by_tile(gb[:, :]), gate[:, x_group(g), D * phase:D * (phase + 1)], bias,
                                       ALU.mult).then_inc(gb_ready, 1)
                    pool.wait_ge(gb_ready, gg + 1)
                    pool.tensor_tensor(by_tile(xg[:, p, :]), by_tile(gb[:, :]), X[:, x_group(g), :],
                                       ALU.add).then_inc(xg_ready, 1)
                else:
                    pool.tensor_tensor(by_tile(xg[:, p, :]), X[:, x_group(g), :], bias, ALU.add).then_inc(xg_ready, 1)

            def add_gated(phase, g, p):
                gg = phase * NG + g
                pool.wait_ge(y_used, gg + 2)
                at = x_group(g) if isinstance(g, int) else bass.ds((gg + NG) % NG * TG, TG)
                pool.tensor_tensor(X[:, at, :], by_tile(yG[:, :]), by_tile(xg[:, p, :]), ALU.add).then_inc(x_updated, 1)

            pool.memset(Qx[:, :, :, :, :], 0.0).then_inc(zeros_ready, 1)
            power(0, 0)
            pool.memset(Vx[:, 0, :, :, :], 0.0).then_inc(zeros_ready, 1)
            pool.wait_ge(ab_ready, 1)
            add_shift(0, 0)
            power(1, 1)
            pool.memset(Vx[:, 1, :, :, :], 0.0).then_inc(zeros_ready, 1)
            add_shift(1, 1)
            power(2, 0)
            pool.memset(yG[:, :], 0.0).then_inc(x_updated, 1)
            subtract_max(0, 1)

            def attention0(g, p):
                add_shift(g + 2, p, 0, g)
                if known(g, 1, NG):
                    if p == 0:
                        pool.wait_ge(gates_in[1], 16 * TB)
                    keep(0, g, p)
                subtract_max(g, 3)
                power(g + 3, 1 - p)
                first = isinstance(g, int) and g == 0
                if not first:
                    add_gated(0, g - 1, 1 - p)
                if known(g, 0, NG - 1):
                    subtract_max(g + 1, 1)
                if first:
                    for i in range(5):
                        pool.wait_ge(x_in[i], 16)
                    pool.wait_ge(gates_in[0], 16 * TB)
                    pool.wait_ge(rows_ready, 1)
                    keep(0, g, p)

            def scale_rows(gg, p):
                pool.wait_ge(rstd_ready, gg + 1)
                if isinstance(gg, int) and gg == 2 * NG + 3:
                    pool.wait_ge(hT_ready, gg)
                else:
                    pool.wait_ge(hT_ready, gg - 1)
                at = x_group(gg % NG) if isinstance(gg, int) else bass.ds(gg % NG * TG, TG)
                pool.tensor_tensor(by_tile(xhat[:, p, :]), X[:, at, :],
                                   rstd[:, p, :].unsqueeze(2).broadcast_to([P, TG, D]), ALU.mult).then_inc(xhat_ready, 1)

            def attention1(g, p):
                power(2 * NG + g + 3, 1 - p)
                scale_rows(2 * NG + g + 3, 1 - p)
                if isinstance(g, int) and g == 0:
                    add_gated(1, 7, 1)
                keep(2, g, p)
                add_shift(2 * NG + g + 2, p, 2, g)

            def mlp(phase):
                def step(g, p):
                    gg = phase * NG + g
                    first = isinstance(g, int) and g == 0
                    if phase == 1 and first:
                        power(gg + 3, 1 - p)
                        pool.wait_ge(gates_in[2], 16 * TB)
                        keep(1, 0, 0)
                        add_gated(0, 7, 1)
                        add_shift(gg + 2, p, phase, g)
                        return
                    if phase == 1 or known(g, 0, 6):
                        add_shift(gg + 2, p, phase, g)
                    if phase == 1 or known(g, 0, 5):
                        power(gg + 3, 1 - p)
                    if phase == 1:
                        add_gated(1, g - 1, 1 - p)
                    keep(phase, g, p)
                return step

            group_steps(pool, attention0)
            group_steps(pool, mlp(1))
            group_steps(pool, attention1)
            group_steps(pool, mlp(3), turns=2)

        @block.vector
        def _(dve):
            links = [0]

            def link(ins):
                links[0] += 1
                ins.then_inc(dve_pre, 1)
                dve.wait_ge(dve_pre, links[0])

            dve.memset(kind[:, 0, 0:2 * NG], 0.0)
            dve.memset(kind[:, 0, 2 * NG:], 1.0)
            dve.memset(kind[:, 1, 0:2 * NG], -1.0)
            dve.memset(kind[:, 1, 2 * NG:], 0.0)
            dve.memset(kind[:, 2, 0:2 * NG], 1e-5)
            dve.memset(kind[:, 2, 2 * NG:], 1e-6)
            dve.memset(Vs[:, :, :], 1.0)
            link(dve.memset(mask[:, :], OFF_BLOCK))
            for b in range(TB):
                last = dve.memset(mask[L * b:L * (b + 1), L * b:L * (b + 1)], 0.0)
            link(last)
            dve.wait_ge(consts_ready, 1)
            link(dve.tensor_reduce(r_sums[:, :], ident[:, :].rearrange("p (n d) -> p n d", d=HD), AX_X, ALU.add))
            link(dve.tensor_reduce(r_mask[:, :], r_sums[:, :].rearrange("p (a r) -> p r a", a=HQ), AX_X, ALU.add))

            def row_stats(gg, tiles=range(TG)):
                for t in tiles:
                    last = dve.bn_stats(stats[:, t, :], X[:, x_tile(gg, t), :])
                if tiles[-1] == TG - 1:
                    last.then_inc(stats_done, 1)

            def aggregate(gg, p, layer0=False):
                for t in range(TG):
                    last = dve.bn_aggr(mv[:, t, :], stats[:, t, :])
                last.then_inc(mv_done, 1)
                dve.wait_ge(mv_done, gg + 1)
                wait(dve, rstd_ready, gg - 1)
                if layer0:
                    dve.tensor_scalar(mk[:, p, :], mv[:, :, 0], -1.0, None, ALU.mult).then_inc(dve_chain, 1)
                    dve.tensor_scalar(v_sb[:, p, :], mv[:, :, 1], 1e-5, None, ALU.add).then_inc(v_ready, 1)
                    return
                dve.scalar_tensor_tensor(out=sqm[:, :], in0=mv[:, :, 0], scalar=kind[:, 0, one(gg)], in1=mv[:, :, 0],
                                         op0=ALU.mult, op1=ALU.mult).then_inc(dve_chain, 1)
                dve.tensor_scalar(mk[:, p, :], mv[:, :, 0], kind[:, 1, one(gg)], None, ALU.mult)
                dve.wait_ge(dve_chain, gg + 1)
                dve.scalar_tensor_tensor(out=v_sb[:, p, :], in0=sqm[:, :], scalar=kind[:, 2, one(gg)], in1=mv[:, :, 1],
                                         op0=ALU.add, op1=ALU.add).then_inc(v_ready, 1)

            def modulate(gg, p, stats_of=None):
                if stats_of is not None:
                    dve.wait_ge(stats_done, stats_of + 1)
                dve.wait_ge(hT_ready, gg + 1)
                wait(dve, h_ready, gg - 1)
                dve.tensor_tensor(by_seq(hA[:, p, :]), by_seq(hT_ps[:, :]),
                                  A[:, seqs(gg)].unsqueeze(2).broadcast_to([P, GB, L]), ALU.mult).then_inc(hA_ready, 1)

            def update(phase, g, p):
                gg = phase * NG + g
                if phase == 2:
                    dve.wait_ge(p1_ready, g + 1)
                    dve.reciprocal(rden1[:, :], den1[:, p, :]).then_inc(rden1_ready, 1)
                    dve.wait_ge(rden1_ready, g + 1)
                dve.wait_ge(y_ready, gg + 1)
                if phase < 2:
                    dve.wait_ge(x_updated, gg + 1)
                    dve.tensor_tensor(by_tile(yG[:, :]), by_tile(y_ps[:, :]), gate[:, x_group(g), D * phase:D * (phase + 1)],
                                      ALU.mult).then_inc(y_used, 1)
                elif phase == 2:
                    dve.wait_ge(xg_ready, gg + 1)
                    for t in range(TG):
                        last = dve.scalar_tensor_tensor(
                            out=X[:, x_tile(g, t), :], in0=y_ps[:, P * t:P * (t + 1)], scalar=rden1[:, t:t + 1],
                            in1=xg[:, p, P * t:P * (t + 1)], op0=ALU.mult, op1=ALU.add)
                    last.then_inc(x_updated, 1)
                else:
                    dve.wait_ge(xg_ready, gg + 1)
                    dve.tensor_tensor(X[:, x_group(g), :], by_tile(y_ps[:, :]), by_tile(xg[:, p, :]),
                                      ALU.add).then_inc(x_updated, 1)

            def row_max(g, t):
                if t % 2 == 0:
                    dve.wait_ge(s_ready, 4 * g + t + 1)
                    S = bank[4]
                else:
                    dve.wait_ge(s_copied, 2 * g + t // 2 + 1)
                    S = Sc
                dve.tensor_reduce(smax[:, t % 2, :], by_seq(S[:, :]), AX_X, ALU.max).then_inc(smax_ready, 1)

            def subtract_max(g, t):
                dve.wait_ge(smax_ready, 4 * g + t + 1)
                dve.tensor_tensor(by_seq(Ss[:, 0, :]), by_seq(bank[4][:, :]),
                                  smax[:, 0, :].unsqueeze(2).broadcast_to([P, TB * HQ, L]),
                                  ALU.subtract).then_inc(s_used[0], 1)

            def turn(g, t):
                dve.wait_ge(s_used[t % 2], 2 * g + t // 2 + 1)
                wait(dve, pt_ready, 4 * g + t - 1)
                dve.transpose(St[:, t % 2, :], Ss[:, t % 2, :]).then_inc(st_ready, 1)

            def o_bank(half):
                return bank[6 + half][:, 0:2 * OW].rearrange("p (n w) -> p n w", w=VW)

            def invert_sums(g, half):
                dve.wait_ge(pv_done, 4 * g + 2 * half + 2)
                dve.reciprocal(rden[:, half, :].unsqueeze(2), o_bank(half)[:, :, HD:VW]).then_inc(rden_ready, 1)

            def normalise(g, p, half):
                dve.wait_ge(rden_ready, 2 * g + half + 1)
                dve.tensor_tensor(On[:, p, 2 * P * half:2 * P * (half + 1)].rearrange("p (n d) -> p n d", d=HD),
                                  o_bank(half)[:, :, 0:HD], rden[:, half, :].unsqueeze(2).broadcast_to([P, 2 * H, HD]),
                                  ALU.mult).then_inc(o_used, 1)

            def softmax1(g, p, stats_of=None):
                dve.wait_ge(s1_ready, g + 1)
                dve.tensor_tensor(by_tile(Ss[:, p, :]), by_tile(bank[7][:, :]),
                                  mask[:, :].unsqueeze(1).broadcast_to([P, TG, P]), ALU.add).then_inc(s1_masked, 1)
                if stats_of is not None:
                    row_stats(stats_of, (0, 1))
                dve.wait_ge(s1_masked, g + 1)
                dve.tensor_reduce(max1[:, :], by_tile(Ss[:, p, :]), AX_X, ALU.max).then_inc(max1_ready, 1)
                if stats_of is not None:
                    row_stats(stats_of, (2, 3))
                    dve.wait_ge(stats_done, stats_of + 1)
                dve.wait_ge(max1_ready, g + 1)
                dve.tensor_scalar(nmax1[:, p, :], max1[:, :], -SCALE1, None, ALU.mult).then_inc(sm1_ready, 1)

            def first_stats(gg):
                dve.wait_ge(x_in[gg], 16)
                row_stats(gg)
                dve.wait_ge(stats_done, gg + 1)
                aggregate(gg, gg % 2, True)

            dve.wait_ge(condT_ready, 1)
            dve.tensor_copy(cT[:, :], bank[1][:, 0:NB]).then_inc(ct_ready, 1)
            first_stats(0)
            dve.wait_ge(exp_c, 1)
            link(dve.tensor_scalar(sT[:, :], eT[:, :], 1.0, None, ALU.add))
            link(dve.reciprocal(eT[:, :], sT[:, :]))
            dve.tensor_tensor(sT[:, :], cT[:, :], eT[:, :], ALU.mult).then_inc(y_used, 1)
            dve.wait_ge(col_in, 16)
            for n, (name, i) in enumerate((("bt", 1), ("bt", 4), ("f1b", 0), ("f2b", 0))):
                dve.tensor_scalar(one_plus[:, n:n + 1], c(name, i), 1.0, None, ALU.add)
            link(dve.tensor_scalar(q_bias[:, :], c("bq"), SCALE0, None, ALU.mult))
            dve.wait_ge(x_in[1], 16)
            row_stats(1)
            def film0(phase, g_, be, sh):
                dve.wait_ge(film_ready, phase + 1)
                at = slice(phase * NB, (phase + 1) * NB)
                scale_ps = bank[6][:, (2 * phase + 1) * NB:(2 * phase + 2) * NB]
                shift_ps = bank[6][:, 2 * phase * NB:(2 * phase + 1) * NB]
                link(dve.tensor_scalar(t_mul[:, :], scale_ps, one_plus[:, phase:phase + 1], c(be), ALU.add, ALU.mult))
                dve.tensor_scalar(A[:, at], scale_ps, one_plus[:, phase:phase + 1], c(g_), ALU.add, ALU.mult)
                dve.scalar_tensor_tensor(out=B[:, at], in0=shift_ps, scalar=c("bt", sh), in1=t_mul[:, :],
                                         op0=ALU.add, op1=ALU.add).then_inc(ab_ready, 1)

            film0(0, "g1", "be1", 0)
            dve.tensor_scalar(k_bias[:, :], r_mask[:, :], c("bk"), None, ALU.mult).then_inc(bias_ready, 1)
            dve.wait_ge(ab_ready, 1)
            modulate(0, 0)
            dve.wait_ge(stats_done, 2)
            aggregate(1, 1, True)
            dve.wait_ge(row_in, 16)
            dve.wait_ge(film_ready, 2)
            dve.tensor_tensor(gate_b[:, 0:D], bank[4][:, 0:D], r("gate0"), ALU.add)
            dve.tensor_tensor(gate_b[:, D:2 * D], bank[4][:, D:2 * D], r("gate1"), ALU.add).then_inc(gate_ready, 1)
            film0(1, "g2", "be2", 3)
            dve.tensor_copy(bcol[:, 0, :], c("bv").broadcast_to([D, D]))
            dve.tensor_copy(bcol[:, 1, :], c("v1b").broadcast_to([D, D]))
            dve.wait_ge(fold_ready, 1)
            dve.tensor_copy(vT[:, :], bank[5][:, 0:D]).then_inc(fold_copied, 1)
            dve.wait_ge(zeros_ready, 1)
            dve.wait_ge(qkv_ready, 1)
            for a in range(HQ):
                at = slice(L * a, L * (a + 1))
                last = dve.tensor_scalar(Qx[at, 0, :, a, :], by_seq(bank[2][at, :]), SCALE0, q_bias[at, :], ALU.mult, ALU.add)
            last.then_inc(q0_placed, 1)
            modulate(1, 1)
            first_stats(2)
            dve.wait_ge(fold_ready, 2)
            dve.tensor_copy(wvp[:, :], bank[5][:, D:2 * D])
            dve.tensor_tensor(r("bproj0"), bank[5][:, 2 * D:3 * D], r("bproj0"), ALU.add)
            dve.tensor_tensor(r("bproj1"), bank[5][:, 3 * D:4 * D], r("bproj1"), ALU.add).then_inc(rows_ready, 1)
            row_max(0, 0)
            subtract_max(0, 0)
            turn(0, 0)
            dve.wait_ge(film_ready, 3)
            for phase, (n_, f) in ((2, ("n1", "f1b")), (3, ("n2", "f2b"))):
                at = slice(phase * NB, (phase + 1) * NB)
                scale_ps = bank[7][:, (2 * phase - 4) * NB:(2 * phase - 3) * NB]
                shift_ps = bank[7][:, (2 * phase - 3) * NB:(2 * phase - 2) * NB]
                dve.tensor_scalar(A[:, at], scale_ps, one_plus[:, phase:phase + 1], c(n_), ALU.add, ALU.mult)
                last = dve.tensor_scalar(B[:, at], shift_ps, c(f, 1), None, ALU.add)
            last.then_inc(ab_ready, 1)
            row_max(0, 1)
            dve.wait_ge(x_in[3], 16)
            dve.wait_ge(x_in[4], 16)

            def attention0(g, p):
                first = isinstance(g, int) and g == 0
                modulate(g + 2, p)
                if not first:
                    invert_sums(g - 1, 1)
                turn(g, 1)
                row_max(g, 2)
                if not first:
                    normalise(g - 1, 1 - p, 1)
                subtract_max(g, 2)
                row_stats(g + 3)
                turn(g, 2)
                dve.wait_ge(stats_done, g + 4)
                row_max(g, 3)
                aggregate(g + 3, 1 - p, True)
                invert_sums(g, 0)
                turn(g, 3)
                if known(g, 0, NG - 1):
                    row_max(g + 1, 0)
                normalise(g, p, 0)
                if known(g, 0, NG - 1):
                    subtract_max(g + 1, 0)
                if not first:
                    if p == 0:
                        dve.wait_ge(gates_in[1], 16 * TB)
                    update(0, g - 1, 1 - p)
                if known(g, 0, NG - 1):
                    turn(g + 1, 0)
                    row_max(g + 1, 1)
                if first:
                    dve.wait_ge(gates_in[0], 16 * TB)

            def mlp(phase):
                def step(g, p):
                    gg = phase * NG + g
                    if isinstance(g, int) and g == 0:
                        if phase == 1:
                            invert_sums(7, 1)
                            normalise(7, 1, 1)
                        else:
                            softmax1(7, 1)
                            update(2, 6, 0)
                    first = isinstance(g, int) and g == 0
                    if phase < 3 or known(g, 0, 5):
                        row_stats(gg + 3)
                    if first and phase == 1:
                        dve.wait_ge(stats_done, gg + 4)
                        aggregate(gg + 3, 1)
                        update(0, 7, 1)
                        dve.wait_ge(gates_in[2], 16 * TB)
                        modulate(gg + 2, p)
                    elif phase < 3 or known(g, 0, 5):
                        modulate(gg + 2, p, gg + 3)
                        aggregate(gg + 3, 1 - p)
                    elif g < 6:
                        modulate(gg + 2, p)
                    if first and phase == 3:
                        update(2, 7, 1)
                    elif not first:
                        update(phase, g - 1, 1 - p)
                return step

            def attention1(g, p):
                if known(g, 1, NG):
                    softmax1(g - 1, 1 - p, 2 * NG + g + 3)
                else:
                    row_stats(2 * NG + g + 3)
                    dve.wait_ge(stats_done, 2 * NG + g + 4)
                aggregate(2 * NG + g + 3, 1 - p)
                if isinstance(g, int) and g == 0:
                    update(1, 7, 1)
                if known(g, 2, NG):
                    update(2, g - 2, p)
                modulate(2 * NG + g + 2, p)

            group_steps(dve, attention0)
            group_steps(dve, mlp(1))
            group_steps(dve, attention1, first=2)
            group_steps(dve, mlp(3), turns=2)
            dve.wait_ge(xg_ready, 4 * NG)
            for half in range(2):
                dve.wait_ge(y_ready, 4 * NG + half)
                lo, hi = 2 * half, 2 * half + 2
                dve.tensor_tensor(X[:, NT - TG + lo:NT - TG + hi, :], by_tile(bank[6 + half][:, :])[:, lo:hi, :],
                                  by_tile(xg[:, 1, :])[:, lo:hi, :], ALU.add).then_inc(x_updated, 1)

        @block.scalar
        def _(act):
            act.dma_start(col[:, :], columns).then_inc(col_in, 16)
            lo, hi = W_AT["Wproj"][0], W_AT["W1_0"][0]
            act.dma_start(W[:, lo:hi], weights[:, lo:hi]).then_inc(wrest_in, 16)
            act.wait_ge(consts_ready, 1)
            act.activation(warm[:, :], minus_half[:, 0:1], ACT.Exp)
            act.wait_ge(ct_ready, 1)
            act.activation(eT[:, :], cT[:, :], ACT.Exp, scale=-1.0).then_inc(exp_c, 1)
            act.dma_start(row[:, :, :], rows.unsqueeze(0).broadcast_to([P, len(R_NAMES), D])).then_inc(row_in, 16)

            def apply(gg, p):
                act.wait_ge(rstd_ready, gg + 1)
                if isinstance(gg, int) and gg == 3 * NG + 3:
                    act.wait_ge(hT_ready, gg)
                else:
                    wait(act, hT_ready, gg - 1)
                for t in range(TG):
                    last = act.activation(xhat[:, p, P * t:P * (t + 1)], X[:, x_tile(gg, t), :], ACT.Identity,
                                          bias=shift[:, p, t:t + 1], scale=rstd[:, p, t:t + 1])
                last.then_inc(xhat_ready, 1)

            def move_q(g, p, k):
                act.wait_ge(qkv_ready, 3 * g + 1)
                wait(act, q_spread[p], 16 * HQ * k)
                act.activation(Qs[:, p, :], bank[2][:, :], ACT.Identity, bias=q_bias[:, :], scale=SCALE0).then_inc(qkv_moved, 1)

            def move_k(g, p, copies=range(HQ)):
                act.wait_ge(qkv_ready, 3 * g + 2)
                wait(act, s_ready, 4 * g - 4)
                for q in copies:
                    last = act.activation(Kx[:, p, q, :], bank[3][:, :], ACT.Identity, bias=k_bias[:, q:q + 1],
                                          scale=r_mask[:, q:q + 1])
                    last.then_inc(kx_ready, 1)

            def move_v(g, p, k):
                act.wait_ge(qkv_ready, 3 * g + 3)
                wait(act, v_stored[p], 16 * k)
                vs = Vs[:, p, :].rearrange("p (n w) -> p n w", w=VW)
                act.activation(vs[:, :, 0:HD], bank[2][:, :].rearrange("p (n d) -> p n d", d=HD),
                               ACT.Copy).then_inc(qkv_moved, 1)

            def exps(g, t):
                tile = 4 * g + t
                act.wait_ge(st_ready, tile + 1)
                wait(act, pv_done, tile - 3)
                act.activation(PT[:, t, :], St[:, t % 2, :], ACT.Exp).then_inc(pt_ready, 1)

            def copy_scores(g, t):
                act.wait_ge(s_ready, 4 * g + t + 1)
                wait(act, s_used[1], 2 * g + t // 2)
                act.activation(Sc[:, :], bank[5][:, :], ACT.Copy).then_inc(s_copied, 1)

            def move_o(g, p):
                act.wait_ge(ot_ready, g + 1)
                act.activation(OTs[:, p, :], bank[1][:, :], ACT.Copy).then_inc(ot_moved, 1)

            def gelus(m, p, chunks=range(NC)):
                for n in chunks:
                    act.wait_ge(u_ready, NC * m + n + 1)
                    bias = c("b1_0" if m_layer[0] == 0 else "b1_1", n)
                    act.activation(gT[:, p, n, :], bank[2 + n][:, :], ACT.Gelu, bias=bias).then_inc(g_ready, 1)

            m_layer = [0]
            apply(0, 0)
            act.wait_ge(bias_ready, 1)
            act.dma_start(W[:, hi:], weights[:, hi:]).then_inc(wmlp_in, 16)
            apply(1, 1)
            act.wait_ge(qkv_ready, 2)
            vs = Vs[:, 0, :].rearrange("p (n w) -> p n w", w=VW)
            for half in range(2):
                act.activation(vs[:, 2 * H * half:2 * H * (half + 1), 0:HD],
                               bank[1][:, 2 * P * half:2 * P * (half + 1)].rearrange("p (n d) -> p n d", d=HD),
                               ACT.Copy).then_inc(qkv_moved, 1)
            act.wait_ge(qkv_ready, 3)
            move_k(0, 0)
            apply(2, 0)
            exps(0, 0)
            copy_scores(0, 1)
            move_q(1, 1, 0)

            def attention0(g, p, k):
                first = isinstance(g, int) and g == 0
                if known(g, 0, NG - 1):
                    move_k(g + 1, 1 - p, (0, 1))
                exps(g, 1)
                copy_scores(g, 3)
                if known(g, 0, NG - 1):
                    move_k(g + 1, 1 - p, (2, 3))
                if known(g, 0, NG - 1):
                    move_v(g + 1, 1 - p, k if p == 0 else k + 1)
                if not first:
                    move_o(g - 1, 1 - p)
                exps(g, 2)
                exps(g, 3)
                if known(g, 0, NG - 1):
                    apply(g + 3, 1 - p)
                if known(g, 0, NG - 1):
                    copy_scores(g + 1, 1)
                    exps(g + 1, 0)
                if known(g, 0, NG - 2):
                    move_q(g + 2, p, k if p == 0 else k + 1)

            attention0(0, 0, 0)
            with act.Fori(0, 2) as i:
                attention0(i * 2 + 1, 1, i)
                attention0(i * 2 + 2, 0, i + 1)
            for g in range(5, NG):
                attention0(g, g % 2, g // 2)

            def mlp(phase):
                def step(g, p):
                    m_layer[0] = phase // 2
                    m = (phase // 2) * NG + g
                    first = isinstance(g, int) and g == 0
                    if first and phase == 3:
                        exps1(7, 1)
                        move_p1(7, 1)
                    gelus(m, p, (0, 1))
                    if first and phase == 1:
                        move_o(7, 1)
                    gelus(m, p, (2, 3))
                    if first and phase == 1:
                        apply(NG + 2, 0)
                    if phase < 3 or not isinstance(g, int) or g < 5:
                        apply(phase * NG + g + 3, 1 - p)
                return step

            def exps1(g, p):
                act.wait_ge(sm1_ready, g + 1)
                act.wait_ge(x_updated, 2 * NG + g)
                for t in range(TG):
                    last = act.activation(St[:, p, P * t:P * (t + 1)], Ss[:, p, P * t:P * (t + 1)], ACT.Exp,
                                          scale=SCALE1, bias=nmax1[:, p, t:t + 1], accum_out=den1[:, p, t:t + 1])
                last.then_inc(p1_ready, 1)

            def move_p1(g, p):
                act.wait_ge(p1T_ready, g + 1)
                act.activation(PT[:, p, :], bank[6][:, :], ACT.Copy).then_inc(p1T_moved, 1)

            def move_qkv1(g, p, which):
                if which == 2 and known(g, 2, NG):
                    act.wait_ge(y_ready, 2 * NG + g - 1)
                act.wait_ge(qkv1_ready, 3 * g + which + 1)
                if which == 0:
                    act.activation(Qs[:, p, :], bank[2][:, :], ACT.Identity, bias=c("q1b")).then_inc(qkv1_moved, 1)
                elif which == 1:
                    act.activation(Kx[:, p, 0, :], bank[3][:, :], ACT.Identity, bias=c("k1b")).then_inc(qkv1_moved, 1)
                else:
                    act.activation(Vs[:, p, 0:GN], bank[4][:, :], ACT.Copy).then_inc(qkv1_moved, 1)

            def attention1(g, p):
                first = isinstance(g, int) and g == 0
                move_qkv1(g, p, 0)
                move_qkv1(g, p, 1)
                if not first:
                    exps1(g - 1, 1 - p)
                move_qkv1(g, p, 2)
                if not first:
                    move_p1(g - 1, 1 - p)

            group_steps(act, mlp(1))
            group_steps(act, attention1, first=2)
            group_steps(act, mlp(3), turns=2)

        @block.tensor
        def _(pe):
            pe.wait_ge(consts_ready, 1)
            pe.wait_ge(cond_in, 16)
            pe.transpose(bank[1][:, 0:NB], c_tok[:, :], ident[:, :]).then_inc(condT_ready, 1)

            def rows_T(gg, p):
                pe.wait_ge(xhat_ready, gg + 1)
                wait(pe, hA_ready, gg)
                for t in range(TG):
                    last = pe.transpose(hT_ps[:, P * t:P * (t + 1)], xhat[:, p, P * t:P * (t + 1)], ident[:, :])
                last.then_inc(hT_ready, 1)

            pe.wait_ge(y_used, 1)
            pe.wait_ge(wt_in, 16)
            for n, i in enumerate((0, 1)):
                last = pe.matmul(bank[6][:, n * NB:(n + 1) * NB], w("Wt", i), sT[:, :], start=True, stop=True)
            last.then_inc(film_ready, 1)
            rows_T(0, 0)
            pe.wait_ge(ab_ready, 1)
            for n, i in enumerate((3, 4)):
                pe.matmul(bank[6][:, (n + 2) * NB:(n + 3) * NB], w("Wt", i), sT[:, :], start=True, stop=True)
            for n, i in enumerate((2, 5)):
                last = pe.matmul(bank[4][:, n * D:(n + 1) * D], sT[:, :], w("Wt", i), start=True, stop=True)
            last.then_inc(film_ready, 1)
            pe.wait_ge(wrest_in, 16)
            pe.transpose(bank[5][:, 0:D], w("v1"), ident[:, :]).then_inc(fold_ready, 1)

            def up(phase, g, p, chunks=range(NC)):
                m = (phase // 2) * NG + g
                pe.wait_ge(h_ready, phase * NG + g + 1)
                for n in chunks:
                    wait(pe, g_ready, NC * (m - 1) + n + 1)
                    last = pe.matmul(bank[2 + n][:, :], w(f"W1_{phase // 2}", n), h[:, p, :], start=True, stop=True)
                    last.then_inc(u_ready, 1)

            def queries0(g, p):
                pe.wait_ge(h_ready, g + 1)
                wait(pe, qkv_moved, 2 * g)
                pe.matmul(bank[2][:, :], w("Wqkv", 0), h[:, p, :], start=True, stop=True).then_inc(qkv_ready, 1)

            def keys0(g, p):
                wait(pe, kx_ready, HQ * g)
                pe.matmul(bank[3][:, :], w("Wqkv", 1), h[:, p, :], start=True, stop=True).then_inc(qkv_ready, 1)

            def values0(g, p):
                pe.wait_ge(qkv_moved, 2 * g + 1)
                for t in range(TG):
                    last = pe.matmul(bank[2][:, P * t:P * (t + 1)], h[:, p, P * t:P * (t + 1)], w("Wqkv", 2),
                                     start=True, stop=True)
                last.then_inc(qkv_ready, 1)

            def scores0(g, p, t):
                tile = 4 * g + t
                if t % 2 == 0:
                    wait(pe, s_used[0], 2 * g + t // 2)
                else:
                    wait(pe, s_copied, 2 * g + t // 2)
                for b in range(TB):
                    at = P * t + L * b
                    last = pe.matmul(bank[4 + t % 2][:, P * b:P * (b + 1)], Qx[:, p, TB * t + b, :, :].rearrange("p a t -> p (a t)"), Kx[:, p, :, at:at + L],
                                     start=True, stop=True)
                last.then_inc(s_ready, 1)

            def weigh0(g, p, t):
                tile = 4 * g + t
                pe.wait_ge(pt_ready, tile + 1)
                if t % 2 == 0:
                    wait(pe, o_used, 2 * g - 1 + t // 2)
                for q in range(HQ):
                    for b in range(TB):
                        at = (t % 2) * OW + q * HQ * VW
                        last = pe.matmul(bank[6 + t // 2][L * b:L * (b + 1), at:at + HQ * VW],
                                         PT[:, t, P * b + L * q:P * b + L * (q + 1)],
                                         Vx[:, p, TB * t + b, :, VW * q:VW * (q + 1)], start=True, stop=True)
                last.then_inc(pv_done, 1)

            def output_T(g, p):
                pe.wait_ge(o_used, 2 * g + 2)
                pe.wait_ge(y_used, g + 1)
                for t in range(TG):
                    last = pe.transpose(bank[1][:, P * t:P * (t + 1)], On[:, p, P * t:P * (t + 1)], ident[:, :])
                last.then_inc(ot_ready, 1)

            def project0(g, p):
                pe.wait_ge(ot_moved, g + 1)
                for t in range(TG):
                    last = pe.matmul(y_ps[:, P * t:P * (t + 1)], OTs[:, p, P * t:P * (t + 1)], w("Wproj"),
                                     start=True, stop=True)
                last.then_inc(y_ready, 1)

            queries0(0, 0)
            for t in range(TG):
                last = pe.matmul(bank[1][:, P * t:P * (t + 1)], h[:, 0, P * t:P * (t + 1)], w("Wqkv", 2), start=True, stop=True)
            last.then_inc(qkv_ready, 1)
            keys0(0, 0)
            rows_T(1, 1)
            for m, name in enumerate(("film1", "film2")):
                for n in range(2):
                    last = pe.matmul(bank[7][:, (2 * m + n) * NB:(2 * m + n + 1) * NB], w(name, n), cT[:, :], start=True, stop=True)
            last.then_inc(film_ready, 1)
            pe.wait_ge(fold_copied, 1)
            pe.matmul(bank[5][:, D:2 * D], vT[:, :], w("proj1"), start=True, stop=True)
            pe.matmul(bank[5][:, 2 * D:3 * D], bcol[:, 0, :], w("Wproj"), start=True, stop=True)
            pe.matmul(bank[5][:, 3 * D:4 * D], bcol[:, 1, :], w("proj1"), start=True, stop=True).then_inc(fold_ready, 1)
            pe.wait_ge(q0_placed, 1)
            pe.wait_ge(kx_ready, HQ)
            scores0(0, 0, 0)
            queries0(1, 1)
            pe.wait_ge(rows_ready, 1)
            scores0(0, 0, 1)

            def attention0(g, p, k):
                first = isinstance(g, int) and g == 0
                rows_T(g + 2, p)
                scores0(g, p, 2)
                if known(g, 0, NG - 1):
                    keys0(g + 1, 1 - p)
                else:
                    pe.wait_ge(wmlp_in, 16)
                    pe.wait_ge(qkv_moved, 2 * NG)
                    up(1, 0, 0, (0, 1))
                pe.wait_ge(v_spread[p], 16 * HQ * (k + 1))
                weigh0(g, p, 0)
                scores0(g, p, 3)
                if known(g, 0, NG - 1):
                    values0(g + 1, 1 - p)
                if not first:
                    output_T(g - 1, 1 - p)
                weigh0(g, p, 1)
                if known(g, 0, NG - 1):
                    pe.wait_ge(q_spread[1 - p], 16 * HQ * (k + 1))
                    pe.wait_ge(kx_ready, HQ * (g + 2))
                    scores0(g + 1, 1 - p, 0)
                if not known(g, 0, NG - 1):
                    pe.wait_ge(s_copied, 2 * NG)
                    pe.wait_ge(s_used[0], 2 * NG)
                    up(1, 0, 0, (2, 3))
                if not first:
                    project0(g - 1, 1 - p)
                if known(g, 0, NG - 1):
                    scores0(g + 1, 1 - p, 1)
                if known(g, 0, NG - 2):
                    queries0(g + 2, p)
                weigh0(g, p, 2)
                weigh0(g, p, 3)

            attention0(0, 0, 0)
            with pe.Fori(0, 2) as i:
                attention0(i * 2 + 1, 1, i)
                attention0(i * 2 + 2, 0, i + 1)
            for g in range(5, NG):
                attention0(g, g % 2, g // 2)

            def down(phase, g, p, y=(y_ps, y_ps)):
                gg, m = phase * NG + g, (phase // 2) * NG + g
                pe.wait_ge(g_ready, NC * (m + 1))
                if phase == 1:
                    pe.wait_ge(y_used, gg + 1)
                elif y[0] is y_ps:
                    pe.wait_ge(x_updated, gg + 1)
                for t in range(TG):
                    if y[0] is not y_ps and t == TG // 2:
                        last.then_inc(y_ready, 1)
                    for n in range(NC):
                        last = pe.matmul(y[t // 2][:, P * t:P * (t + 1)], gT[:, p, n, P * t:P * (t + 1)],
                                         w(f"W2_{phase // 2}", n), start=(n == 0), stop=(n == NC - 1))
                last.then_inc(y_ready, 1)

            def qkv1(g, p):
                pe.wait_ge(h_ready, 2 * NG + g + 1)
                wait(pe, qkv1_moved, 3 * g)
                pe.matmul(bank[2][:, :], w("q1"), h[:, p, :], start=True, stop=True).then_inc(qkv1_ready, 1)
                pe.matmul(bank[3][:, :], w("k1"), h[:, p, :], start=True, stop=True).then_inc(qkv1_ready, 1)
                for t in range(TG):
                    last = pe.matmul(bank[4][:, P * t:P * (t + 1)], h[:, p, P * t:P * (t + 1)], wvp[:, :],
                                     start=True, stop=True)
                last.then_inc(qkv1_ready, 1)

            def scores1(g, p):
                pe.wait_ge(qkv1_moved, 3 * g + 2)
                wait(pe, s1_masked, g)
                for t in range(TG):
                    at = slice(P * t, P * (t + 1))
                    last = pe.matmul(bank[7][:, at], Qs[:, p, at], Kx[:, p, 0, at], start=True, stop=True)
                last.then_inc(s1_ready, 1)

            def probs_T(g, p):
                pe.wait_ge(p1_ready, g + 1)
                for t in range(TG):
                    last = pe.transpose(bank[6][:, P * t:P * (t + 1)], St[:, p, P * t:P * (t + 1)], ident[:, :])
                last.then_inc(p1T_ready, 1)

            def values1(g, p):
                pe.wait_ge(p1T_moved, g + 1)
                pe.wait_ge(x_updated, 2 * NG + g + 1)
                for t in range(TG):
                    at = slice(P * t, P * (t + 1))
                    last = pe.matmul(y_ps[:, at], PT[:, p, at], Vs[:, p, at], start=True, stop=True)
                last.then_inc(y_ready, 1)

            def mlp(phase):
                def step(g, p):
                    gg = phase * NG + g
                    first = isinstance(g, int) and g == 0
                    if first and phase == 1:
                        output_T(7, 1)
                    elif first:
                        up(phase, g, p, (0, 1))
                        values1(6, 0)
                        up(phase, g, p, (2,))
                        probs_T(7, 1)
                        up(phase, g, p, (3,))
                    elif not (phase == 1 and isinstance(g, int) and g == 1):
                        up(phase, g, p)
                    if first and phase == 1:
                        up(1, 1, 1, (0, 1))
                        project0(7, 1)
                        up(1, 1, 1, (2, 3))
                    if phase < 3 or not isinstance(g, int) or g < 6:
                        rows_T(gg + 2, p)
                    if not first:
                        down(phase, g - 1, 1 - p)
                    elif phase == 3:
                        values1(7, 1)
                return step

            def attention1(g, p):
                first = isinstance(g, int) and g == 0
                if first:
                    pe.wait_ge(g_ready, NC * NG)
                qkv1(g, p)
                if known(g, 2, NG):
                    values1(g - 2, p)
                if first:
                    down(1, 7, 1)
                rows_T(2 * NG + g + 2, p)
                scores1(g, p)
                if known(g, 1, NG):
                    probs_T(g - 1, 1 - p)

            group_steps(pe, mlp(1), first=2)
            group_steps(pe, attention1, first=2)
            group_steps(pe, mlp(3), turns=2)
            down(3, 7, 1, (bank[6], bank[7]))


def kernel(x, cond_1024, L0_cond_Wqkv, L0_cond_bqkv, L0_cond_Wproj, L0_cond_bproj, L0_cond_W1, L0_cond_b1,
           L0_cond_W2, L0_cond_b2, L0_cond_Wt, L0_cond_bt, L0_cond_g1, L0_cond_be1, L0_cond_g2, L0_cond_be2,
           L1_cond_norm1_w, L1_cond_film1_w, L1_cond_film1_b, L1_cond_q_w, L1_cond_q_b, L1_cond_k_w, L1_cond_k_b,
           L1_cond_v_w, L1_cond_v_b, L1_cond_proj_w, L1_cond_proj_b, L1_cond_norm2_w, L1_cond_film2_w,
           L1_cond_film2_b, L1_cond_mlp_w1, L1_cond_mlp_b1, L1_cond_mlp_w2, L1_cond_mlp_b2):
    import numpy as np
    import concourse.bacc as bacc
    from concourse.bass_utils import run_bass_kernel_spmd

    def by_a(m):
        return m.reshape(m.shape[:-1] + (HQ, HQ, HD)).swapaxes(-3, -2).reshape(m.shape)

    def chunks(m):
        return m.reshape(-1, P, m.shape[-1]).swapaxes(0, 1).reshape(P, -1)

    wqkv = np.asarray(L0_cond_Wqkv).reshape(D, 3, D)
    bqkv = np.asarray(L0_cond_bqkv).reshape(3, D)
    bt = np.asarray(L0_cond_bt).reshape(6, D)
    ws = {"Wt": L0_cond_Wt, "film1": L1_cond_film1_w, "film2": L1_cond_film2_w, "Wproj": L0_cond_Wproj,
          "v1": L1_cond_v_w, "proj1": L1_cond_proj_w, "Wqkv": by_a(wqkv).reshape(D, 3 * D), "W1_0": L0_cond_W1,
          "W2_0": chunks(np.asarray(L0_cond_W2)), "q1": L1_cond_q_w, "k1": L1_cond_k_w, "W1_1": L1_cond_mlp_w1,
          "W2_1": chunks(np.asarray(L1_cond_mlp_w2))}
    cs = {"bt": bt, "g1": L0_cond_g1, "be1": L0_cond_be1, "g2": L0_cond_g2, "be2": L0_cond_be2, "bq": by_a(bqkv[0]),
          "bk": by_a(bqkv[1]), "bv": bqkv[2], "b1_0": L0_cond_b1, "n1": L1_cond_norm1_w, "n2": L1_cond_norm2_w,
          "f1b": L1_cond_film1_b, "f2b": L1_cond_film2_b, "q1b": L1_cond_q_b, "k1b": L1_cond_k_b, "v1b": L1_cond_v_b,
          "b1_1": L1_cond_mlp_b1}
    rs = {"gate0": bt[2], "gate1": bt[5], "bproj0": L0_cond_bproj, "b2_0": L0_cond_b2, "bproj1": L1_cond_proj_b,
          "b2_1": L1_cond_mlp_b2}
    arrays = {
        "x": np.ascontiguousarray(np.asarray(x).reshape(NB * L, D)),
        "cond": np.ascontiguousarray(np.asarray(cond_1024)),
        "weights": np.ascontiguousarray(np.concatenate([np.asarray(ws[n]) for n, _ in W_NAMES], axis=1)),
        "columns": np.ascontiguousarray(np.concatenate([np.asarray(cs[n]).reshape(-1, D) for n, _ in C_NAMES], axis=0).T),
        "rows": np.ascontiguousarray(np.stack([np.asarray(rs[n]) for n in R_NAMES])),
    }
    nc = bacc.Bacc("TRN2", target_bir_lowering=False, num_devices=1)
    aps = [nc.dram_tensor(n, a.shape, mybir.dt.from_np(a.dtype), kind="ExternalInput").ap() for n, a in arrays.items()]
    out = nc.dram_tensor("out", (NB * L, D), F32, kind="ExternalOutput").ap()
    build(nc, *aps, out)
    result = run_bass_kernel_spmd(nc, [arrays], core_ids=[0])
    return result.results[0]["out"].reshape(NB, L, D)
```
